# Optimizing a Trainium2 kernel written in Bass

```python
import numpy as np
import jax
import jax.numpy as jnp

def _softmax(x, axis=-1):
    return jax.nn.softmax(x, axis=axis)

def _gelu(x):
    return jax.nn.gelu(x, approximate=True)

def _silu(x):
    return jax.nn.silu(x)

def _sigmoid(x):
    return jax.nn.sigmoid(x)

def _layernorm(x, axis=-1, eps=1e-05):
    m = jnp.mean(x, axis=axis, keepdims=True)
    v = jnp.var(x, axis=axis, keepdims=True)
    return (x - m) / jnp.sqrt(v + eps)

def _scatter_add(tgt, idx, src, axis=0):
    return tgt.at[idx].add(src)

def _segment_sum(src, seg, n):
    return jax.ops.segment_sum(src, seg, n)
kernel_name = 'mk_recurrent_d1_jaxref_r2_e43003'

def setup_inputs(seed: int=0):
    np.random.seed(seed)
    _w = jnp.asarray

    def _L0_attn_setup():
        import jax, jax.numpy as jnp
        import numpy as np
        B, C, L = (64, 256, 2048)
        key = jax.random.key(seed)
        x = jax.random.normal(key, (B, C, L), dtype=jnp.float32)
        return {'x': x}
    _L0_attn_in = _L0_attn_setup()

    def _L0_ffn_setup():
        import jax, jax.numpy as jnp
        import numpy as np

        def sparsemax(z):
            E = z.shape[-1]
            z_sorted = -jnp.sort(-z, axis=-1)
            z_cum = jnp.cumsum(z_sorted, axis=-1)
            k = jnp.arange(1, E + 1, dtype=z.dtype)
            support = 1.0 + k * z_sorted > z_cum
            k_z = jnp.sum(support, axis=-1, keepdims=True)
            tau_sum = jnp.take_along_axis(z_cum, k_z.astype(jnp.int32) - 1, axis=-1)
            tau = (tau_sum - 1.0) / k_z.astype(z.dtype)
            return jnp.maximum(z - tau, 0.0)
        key = jax.random.key(seed)
        ks = jax.random.split(key, 6)
        B, S, D_IN, D_OUT, E, R = (8, 1024, 2048, 2048, 8, 16)
        x = jax.random.normal(ks[0], (B, S, D_IN), dtype=jnp.float32)
        W_base = jax.random.normal(ks[1], (D_OUT, D_IN), dtype=jnp.float32) * D_IN ** (-0.5)
        b_base = jax.random.normal(ks[2], (D_OUT,), dtype=jnp.float32) * 0.01
        W_router = jax.random.normal(ks[3], (E, D_IN), dtype=jnp.float32) * D_IN ** (-0.5)
        b_router = jnp.zeros((E,), dtype=jnp.float32)
        lora_A = jax.random.normal(ks[4], (E, D_IN, R), dtype=jnp.float32) * D_IN ** (-0.5)
        lora_B = jnp.zeros((E, R, D_OUT), dtype=jnp.float32)
        return {'x': x, 'W_base': W_base, 'b_base': b_base, 'W_router': W_router, 'b_router': b_router, 'lora_A': lora_A, 'lora_B': lora_B}
    _L0_ffn_in = _L0_ffn_setup()
    _d = {'L0_attn_x': _L0_attn_in['x'], 'L0_ffn_W_base': _L0_ffn_in['W_base'], 'L0_ffn_b_base': _L0_ffn_in['b_base'], 'L0_ffn_W_router': _L0_ffn_in['W_router'], 'L0_ffn_b_router': _L0_ffn_in['b_router'], 'L0_ffn_lora_A': _L0_ffn_in['lora_A'], 'L0_ffn_lora_B': _L0_ffn_in['lora_B']}
    _x0 = _d['L0_attn_x']
    _d['L0_attn_x'] = jax.random.normal(jax.random.fold_in(jax.random.key(seed), 1), (2, 2048, 2048), dtype=_x0.dtype)
    del _x0
    return _d

def reference(L0_attn_x, L0_ffn_W_base, L0_ffn_b_base, L0_ffn_W_router, L0_ffn_b_router, L0_ffn_lora_A, L0_ffn_lora_B):

    def _L0_attn_ref(x):
        import jax, jax.numpy as jnp
        import numpy as np
        B, C, L = (64, 256, 2048)
        b, c, l = x.shape
        q = jnp.transpose(x, (2, 0, 1))
        scale = jnp.asarray(c, x.dtype) ** 0.5
        scores = jnp.einsum('lnc,lmc->lnm', q, q) / scale
        prob = jax.nn.softmax(scores, axis=-1)
        msg = jnp.einsum('lnm,lmc->lnc', prob, q)
        return x + jnp.transpose(msg, (1, 2, 0))

    def _L0_ffn_ref(x, W_base, b_base, W_router, b_router, lora_A, lora_B):
        import jax, jax.numpy as jnp
        import numpy as np

        def sparsemax(z):
            E = z.shape[-1]
            z_sorted = -jnp.sort(-z, axis=-1)
            z_cum = jnp.cumsum(z_sorted, axis=-1)
            k = jnp.arange(1, E + 1, dtype=z.dtype)
            support = 1.0 + k * z_sorted > z_cum
            k_z = jnp.sum(support, axis=-1, keepdims=True)
            tau_sum = jnp.take_along_axis(z_cum, k_z.astype(jnp.int32) - 1, axis=-1)
            tau = (tau_sum - 1.0) / k_z.astype(z.dtype)
            return jnp.maximum(z - tau, 0.0)
        base_out = jnp.einsum('bsd,od->bso', x, W_base) + b_base
        logits = jnp.einsum('bsd,ed->bse', x, W_router) + b_router
        weights = sparsemax(logits)
        h = jnp.einsum('bsd,edr->bser', x, lora_A)
        expert_out = jnp.einsum('bser,bse,ero->bso', h, weights, lora_B)
        return base_out + expert_out
    x = L0_attn_x
    xn = _layernorm(x, axis=-1)
    s = _L0_attn_ref(xn)
    g = _silu(_L0_ffn_ref(xn, L0_ffn_W_base, L0_ffn_b_base, L0_ffn_W_router, L0_ffn_b_router, L0_ffn_lora_A, L0_ffn_lora_B))
    x = x + s * g
    return x

_drawn_inputs = setup_inputs


def setup_inputs(seed=0):
    import zlib

    import numpy as np

    out = dict(_drawn_inputs(seed))
    spreads = {'L0_ffn_b_router': (0.0, 0.658), 'L0_ffn_lora_B': (0.0, 0.1)}
    factors = {'L0_ffn_b_base': 8.0}
    for name, (base, spread) in spreads.items():
        noise = np.random.default_rng([zlib.crc32(name.encode()), seed]).standard_normal(out[name].shape)
        drawn = base * np.exp(spread * noise) if base else spread * noise
        out[name] = jnp.asarray(drawn.astype(out[name].dtype))
    for name, factor in factors.items():
        out[name] = (out[name] * factor).astype(out[name].dtype)
    return out
```

```python
def build(nc, x, W, b_base, Wr, b_router, lora_A, lora_B, out, g_dram):
    from contextlib import ExitStack

    import concourse.bass as bass
    from concourse import mybir

    F32, F16, BF16, U32 = mybir.dt.float32, mybir.dt.float16, mybir.dt.bfloat16, mybir.dt.uint32
    ALU = mybir.AluOpType
    ACT = mybir.ActivationFunctionType
    AX = mybir.AxisListType
    ds = bass.ds

    P = 128
    _, C, L = x.shape
    O = W.shape[0]
    E, _, R = lora_A.shape
    ER = E * R
    KB = L // P
    CH = 512
    NQ = L // CH
    BPQ = CH // P
    HALF = KB // 2
    PAIRS = C // P
    AUG = ER + E
    XS = 2.0 ** 8
    EPS = 1e-5
    AHEAD = 1
    EXP = 1 << 23

    B_PAIRS = 8
    B_STATS = PAIRS // B_PAIRS
    D_STEPS = B_PAIRS
    D_PAIRS = (PAIRS - B_PAIRS) // D_STEPS
    B_TILES = 2 * B_PAIRS

    WT = O // P
    IT_R, IT_A, IT_AT = WT, WT + 1, WT + 2
    ITEMS = WT + 3
    W_GROUPS = 4 * WT + 8
    ZG = W_GROUPS + 8
    PX = 8

    xr = x.rearrange("b c l -> (b c) l")
    outr = out.rearrange("b c l -> (b c) l")

    with ExitStack() as ctx:
        def sb(name, shape, dt):
            return ctx.enter_context(nc.sbuf_tensor(name, shape, dt))

        def sem(name):
            return ctx.enter_context(nc.semaphore(name))

        w_hi = sb("w_hi", [P, KB, O], F16)
        w_lo = sb("w_lo", [P, KB, O], F16)
        a_hi = sb("a_hi", [P, KB, AUG], F16)
        a_lo = sb("a_lo", [P, KB, AUG], F16)
        b_lora = sb("b_lora", [ER, O], F32)
        unscale = sb("unscale", [P, O], BF16)
        bias = sb("bias", [P, O], F32)
        unscale_aug = sb("unscale_aug", [P, AUG], F32)
        bias_r = sb("bias_r", [P, E], F32)
        xt_hi = sb("xt_hi", [P, 2, KB, P], F16)
        xt_lo = sb("xt_lo", [P, 2, KB, P], F16)
        xc = sb("xc", [P, 2, CH], F32)
        zs = sb("zs", [P, 2, CH], F32)
        ident = sb("ident", [P, P], F32)
        mean = sb("mean", [P, 2, PAIRS + 1], F32)
        rs = sb("rs", [P, 2, PAIRS + 1], F32)
        rstd = sb("rstd", [P, 2, PAIRS + 1], F32)
        nmr = sb("nmr", [P, 2, PAIRS + 1], F32)
        pair_tab = sb("pair_tab", [P, 2, 2, 2], F32)
        bn = sb("bn", [P, 2, NQ, 6], F32)
        mv = sb("mv", [P, 2, 2], F32)
        vare = sb("vare", [P, 2], F32)
        std = sb("std", [P, 2], F32)
        r2 = sb("r2", [P, 2], F32)
        l1 = sb("l1", [P, ITEMS], F32)
        eb = sb("eb", [P, ITEMS], U32)
        sc = sb("sc", [P, ITEMS], U32)
        us = sb("us", [P, ITEMS], U32)
        isc = sb("isc", [P, ITEMS], F32)
        kio = sb("kio", [P, E], F32)
        one8 = sb("one8", [P, E], F32)
        haug = sb("haug", [P, AUG], F32)
        dcol = sb("dcol", [P, 2 * KB], F32)
        ex = sb("ex", [P, 4 * KB], F32)
        hw = sb("hw", [P, ER], F32)
        hwT = sb("hwT", [ER, P], F32)
        sp_z = sb("sp_z", [P, E], F32)
        sp_s = sb("sp_s", [P, E], F32)
        sp_c = sb("sp_c", [P, E], F32)
        sp_k = sb("sp_k", [P, E], F32)
        sp_u = sb("sp_u", [P, E], F32)
        sp_v = sb("sp_v", [P, E], F32)
        sp_w = sb("sp_w", [P, E], F32)
        sp_n = sb("sp_n", [P, 4], F32)

        work = sb("work", [P, 4 * L + 1024], F32)
        stage = [work[:, (2 + k) % 4 * L:((2 + k) % 4 + 1) * L] for k in range(4)]
        a_grouped = stage[(WT - 1) % 4]
        diag = [work[:, 4 * L + k * CH:4 * L + (k + 1) * CH] for k in range(2)]
        acc = [work[:, n * L:(n + 1) * L] for n in range(2)]
        xp = [work[:, (2 + n) * L:(3 + n) * L] for n in range(2)]
        dtmp = work[:, 4 * L:4 * L + 1024]
        prow = xp
        xa = [work[:, k * CH:(k + 1) * CH] for k in range(2)]
        xo = [work[:, (2 + k) * CH:(3 + k) * CH] for k in range(2)]
        na = [work[:, (4 + k) * CH:(5 + k) * CH] for k in range(2)]
        gx = [work[:, (6 + k) * CH:(7 + k) * CH] for k in range(2)]
        ones = sb("ones", [P, P], F32)

        zb = [ctx.enter_context(nc.psum_tensor(f"zb{k}", [P, CH], F32)) for k in range(4)]
        tp = [ctx.enter_context(nc.psum_tensor(f"tp{k}", [P, CH], F32)) for k in range(2)]
        hb = ctx.enter_context(nc.psum_tensor("hb", [P, CH], F32))
        hwb = ctx.enter_context(nc.psum_tensor("hwb", [P, CH], F32))

        s_const = sem("s_const")
        s_ident = sem("s_ident")
        s_x0 = sem("s_x0")
        s_item = [sem(f"s_item{k}") for k in range(4)]
        s_l1 = sem("s_l1")
        s_scaled = sem("s_scaled")
        s_wtp = sem("s_wtp")
        s_whi = sem("s_whi")
        s_itdone = sem("s_itdone")
        s_diag = sem("s_diag")
        s_at = sem("s_at")
        s_zused = sem("s_zused")
        s_aug = sem("s_aug")
        s_augu = sem("s_augu")
        s_var = sem("s_var")
        s_std = sem("s_std")
        s_rstd = sem("s_rstd")
        s_xc = [sem(f"s_xc{k}") for k in range(2)]
        s_xn = sem("s_xn")
        s_tp = sem("s_tp")
        s_hi = sem("s_hi")
        s_lo = sem("s_lo")
        s_h = sem("s_h")
        s_hw = sem("s_hw")
        s_hwtp = sem("s_hwtp")
        s_hwT = sem("s_hwT")
        s_z = sem("s_z")
        s_zb = sem("s_zb")
        s_g = sem("s_g")
        s_gst = [sem(f"s_gst{k}") for k in range(2)]
        s_xp = sem("s_xp")
        s_xnp = sem("s_xnp")
        s_acc = sem("s_acc")
        s_dsum = sem("s_dsum")
        s_d = sem("s_d")
        s_e = sem("s_e")
        s_fin = sem("s_fin")
        s_fl = [sem(f"s_fl{k}") for k in range(2)]
        s_nrm = sem("s_nrm")
        s_out = [sem(f"s_out{k}") for k in range(2)]

        TILES_D = 2 * D_PAIRS
        early = [("early", n, q) for n in range(2) for q in range(NQ)]
        units, per_tile = [], {}
        for t in range(TILES_D):
            share = [early.pop(0) for _ in range(2 * NQ // TILES_D)]
            per_tile[t] = []
            for group in (share[0:2], share[2:3], [("tile", t, 0)], [("tile", t, 1)], share[3:] + [("tile", t, 2)],
                          [("tile", t, 3)]):
                per_tile[t].append(range(len(units), len(units) + len(group)))
                units += group
        assert not early and len(units) == TILES_D * NQ + 2 * NQ
        UNITS = len(units)
        load_count, total = [], [0, 0]
        for k, u in enumerate(units):
            total[k % 2] += 48 if u[0] == "early" else 32
            load_count.append(total[k % 2])
        fin0 = 2

        def tile_of(i, t):
            return B_TILES + TILES_D * i + t, B_PAIRS + D_PAIRS * i + t // 2, t % 2

        def next_of(j, n):
            return (j, 1) if n == 0 else (j + 1, 0)

        def rows(n, j):
            return ds(j * P + n * C, P)

        def cols(q):
            return slice(q * CH, (q + 1) * CH)

        def unit_place(i, u):
            kind, t, q = u
            if kind == "early":
                return t, i, q, None
            T, j, n = tile_of(i, t)
            return n, j, q, T

        block = ctx.enter_context(nc.Block())

        @block.sync
        def _(sp):
            for n in range(2):
                sp.dma_start(stage[2 + n], xr[rows(n, 0), :]).then_inc(s_x0, 16)
            for m in range(IT_AT):
                if m in (2, 3):
                    sp.wait_ge(s_var, 1)
                if m >= 4:
                    sp.wait_ge(s_itdone, m - 3)
                if m < WT:
                    sp.dma_start(stage[m % 4], W[m * P:(m + 1) * P, :]).then_inc(s_item[m % 4], 16)
                elif m == IT_R:
                    sp.dma_start(stage[m % 4][0:E, :], Wr).then_inc(s_item[m % 4], 16)
                else:
                    sp.dma_start(stage[m % 4].rearrange("p (e v) -> p e v", e=E),
                                 lora_A.rearrange("e (p k) r -> p e (k r)", p=P)).then_inc(s_item[m % 4], 16)
                if m == 3:
                    sp.dma_start(b_lora[:, :], lora_B.rearrange("e r o -> (e r) o")).then_inc(s_const, 16)
                    sp.dma_start(bias[:, :], b_base.rearrange("(a o) -> a o", a=1).to_broadcast([P, O]))\
                        .then_inc(s_const, 16)
                    sp.dma_start(bias_r[:, :], b_router.rearrange("(a e) -> a e", a=1).to_broadcast([P, E]))\
                        .then_inc(s_const, 16)

            def load_chunk(T, j, n, q):
                if T is not None:
                    sp.wait_ge(s_tp, 4 * T + q - 1)
                sp.dma_start(xc[:, q % 2, :], xr[rows(n, j), cols(q)]).then_inc(s_xc[q % 2], 16)

            load_chunk(None, 0, 0, 0)
            load_chunk(None, 0, 0, 1)
            load_chunk(0, 0, 0, 2)
            load_chunk(0, 0, 0, 3)

            def load_pair(p):
                sp.wait_ge(s_acc, AHEAD + p)
                for n in range(2):
                    sp.dma_start(xp[n], xr[rows(n, p), :]).then_inc(s_xp, 16)

            sp.wait_ge(s_zused, ZG)
            sp.wait_ge(s_augu, 2)
            with sp.Fori(0, B_PAIRS) as i:
                for n in range(2):
                    T = 2 * i + n
                    nj, nn = next_of(i, n)
                    load_pair(B_STATS * i + n)
                    for q in range(NQ):
                        load_chunk(T + 1, nj, nn, q)

            for k in range(2):
                sp.wait_ge(s_gst[k], AHEAD + 16 * B_TILES * 2)

            def load_unit(i, k, ahead=0):
                n, j, q, _ = unit_place(i, units[k])
                b = k % 2
                down = ahead * P
                sp.dma_start(xa[b], xr[down:, :][rows(n, j), cols(q)]).then_inc(s_fl[b], 16)
                sp.dma_start(xo[b], xr[down:, :][rows(1 - n, j), cols(q)]).then_inc(s_fl[b], 16)
                if units[k][0] == "early":
                    sp.dma_start(gx[b], g_dram[down:, :][ds(j * P + n * B_PAIRS * P, P), cols(q)])\
                        .then_inc(s_fl[b], 16)

            def store_unit(i, k):
                n, j, q, _ = unit_place(i, units[k])
                sp.wait_ge(s_fin, fin0 + UNITS * i + k + 1)
                sp.dma_start(outr[rows(n, j), cols(q)], na[k % 2]).then_inc(s_out[k % 2], 16)
                if k + 2 < UNITS:
                    load_unit(i, k + 2)
                else:
                    load_unit(i, k + 2 - UNITS, 1)

            sp.wait_ge(s_fin, fin0)
            load_unit(0, 0)
            load_unit(0, 1)
            with sp.Fori(0, D_STEPS) as i:
                for t in range(TILES_D):
                    T, j, n = tile_of(i, t)
                    nj, nn = next_of(j, n)
                    e0, e1, f0, f1, f2, f3 = per_tile[t]

                    def load_next(q):
                        sp.wait_ge(s_tp, PX + 4 * (T + 1) + q - 1)
                        sp.dma_start(xc[:, q % 2, :], xr[rows(nn, nj), cols(q)]).then_inc(s_xc[q % 2], 16)

                    for k in e0:
                        store_unit(i, k)
                    load_next(2)
                    for k in e1:
                        store_unit(i, k)
                    load_next(3)
                    for group in (f0, f1, f2, f3):
                        for k in group:
                            store_unit(i, k)
            for k in range(2):
                sp.wait_ge(s_fl[k], total[k] * D_STEPS + load_count[k])
                sp.wait_ge(s_out[k], AHEAD + 16 * D_STEPS * UNITS // 2)

        @block.gpsimd
        def _(pool):
            nc.gpsimd.memset(ident[:, :], 0.0).then_inc(s_ident, 1)
            nc.gpsimd.memset(ones[:, :], 1.0).then_inc(s_ident, 1)
            nc.gpsimd.memset(one8[:, :], 1.0).then_inc(s_ident, 1)
            for e in range(E):
                nc.gpsimd.memset(kio[:, e:e + 1], float(e + 1)).then_inc(s_ident, 1)
            for s in (s_hw, s_hwT, s_hwtp, s_z, s_acc, *s_gst, *s_out):
                nc.gpsimd.nop().then_inc(s, AHEAD)
            for tab in (mean, rs):
                nc.gpsimd.memset(tab[:, :, :], 0.0).then_inc(s_ident, 1)
            pool.wait_ge(s_ident, 5 + E)
            nc.gpsimd.affine_select(out=ident[:, :], in_=ident[:, :], compare_op=ALU.not_equal, fill=1.0,
                                    base=0, pattern=[[-1, P]], channel_multiplier=1).then_inc(s_ident, 1)

        IDENT = 6 + E

        def w_dst(parts, m, q):
            if m < WT:
                return parts[0][:, 4 * q:4 * q + 4, m * P:(m + 1) * P]
            return parts[1][:, 4 * q:4 * q + 4, 0:ER]

        def group_of(m):
            return 4 * m if m < IT_R else 4 * (m - 1)

        @block.scalar
        def _(act):
            junk = zs[:, :, :].rearrange("p a b -> p (a b)").bitcast(BF16)

            def row_sums(m):
                np_ = E if m == IT_R else P
                if m < IT_AT:
                    act.wait_ge(s_item[m % 4], 16 * (m // 4 + 1))
                else:
                    act.wait_ge(s_at, 1)
                act.drain()
                nc.scalar.activation(junk[0:np_, :], stage[m % 4][0:np_, :], ACT.Abs,
                                     accum_out=l1[0:np_, m:m + 1]).then_inc(s_l1, 1)

            def root():
                nc.scalar.activation(std[:, :], vare[:, :], ACT.Sqrt).then_inc(s_std, 1)

            act.wait_ge(s_var, 1)
            root()
            row_sums(0)
            for m in range(ITEMS):
                nxt = m + 1
                if nxt < IT_A:
                    row_sums(nxt)
                if m == IT_R:
                    act.wait_ge(s_aug, 1)
                    nc.scalar.activation(a_hi[:, :, ER:AUG], hb[:, 0:P].rearrange("p (k e) -> p k e", e=E),
                                         ACT.Copy).then_inc(s_whi, 1)
                elif m == IT_A:
                    row_sums(IT_AT)
                else:
                    for q in range(4):
                        g = group_of(m) + q
                        act.wait_ge(s_wtp, g + 1)
                        nc.scalar.activation(w_dst((w_hi, a_hi), m, q),
                                             zb[g % 4][:, :].rearrange("p (k o) -> p k o", k=4),
                                             ACT.Copy).then_inc(s_whi, 1)

            def hi_part(T, n, q, px):
                act.wait_ge(s_tp, px + 4 * T + q + 1)
                if q == 0 and not isinstance(T, int):
                    act.wait_ge(s_z, AHEAD + 4 * (T - 1))
                nc.scalar.activation(xt_hi[:, n, 4 * q:4 * q + 4, :],
                                     tp[q % 2][:, :].rearrange("p (k r) -> p k r", k=4),
                                     ACT.Copy).then_inc(s_hi, 1)

            for q in range(4):
                hi_part(0, 0, q, 0)

            def hwT_out(T):
                act.wait_ge(s_hwtp, AHEAD + T + 1)
                act.wait_ge(s_z, AHEAD + 4 * T)
                nc.scalar.activation(hwT[:, :], hwb[0:ER, 0:P], ACT.Copy).then_inc(s_hwT, 1)

            def silu(T, q):
                act.wait_ge(s_zb, 4 * T + q + 1)
                nc.scalar.activation(zs[:, q % 2, :], zs[:, q % 2, :], ACT.Silu).then_inc(s_g, 1)

            def store_g(T, n, j, q):
                act.wait_ge(s_g, 4 * T + q + 1)
                act.dma_start(g_dram[ds(j * P + n * B_PAIRS * P, P), cols(q)], zs[:, q % 2, :])\
                    .then_inc(s_gst[q % 2], 16)

            def pair_root(p):
                act.wait_ge(s_var, p + 2)
                root()

            def pair_norm(p):
                act.wait_ge(s_rstd, p + 2)
                for n in range(2):
                    nc.scalar.activation(xp[n], xp[n], ACT.Identity, scale=r2[:, n:n + 1],
                                         bias=std[:, n:n + 1]).then_inc(s_xnp, 1)

            with act.Fori(0, B_PAIRS) as i:
                for n in range(2):
                    T = 2 * i + n
                    p = B_STATS * i + n
                    pair_root(p)
                    pair_norm(p)
                    hi_part(T + 1, 1 - n, 0, 0)
                    hi_part(T + 1, 1 - n, 1, 0)
                    hwT_out(T)
                    hi_part(T + 1, 1 - n, 2, 0)
                    silu(T, 0)
                    silu(T, 1)
                    store_g(T, n, i, 0)
                    store_g(T, n, i, 1)
                    hi_part(T + 1, 1 - n, 3, 0)
                    silu(T, 2)
                    store_g(T, n, i, 2)
                    silu(T, 3)
                    store_g(T, n, i, 3)

            act.wait_ge(s_d, 1)
            nc.scalar.activation(ex[:, :], ex[:, :], ACT.Exp).then_inc(s_e, 1)

            def norm_unit(i, k):
                n, j, q, _ = unit_place(i, units[k])
                b = k % 2
                act.wait_ge(s_fl[b], total[b] * i + load_count[k])
                act.wait_ge(s_out[b], AHEAD + 16 * (UNITS // 2 * i + k // 2))
                f = pair_tab[:, 0 if units[k][0] == "early" else 1]
                nc.scalar.activation(na[b], xa[b], ACT.Identity, scale=f[:, 0, n:n + 1], bias=f[:, 1, n:n + 1])
                nc.scalar.activation(xo[b], xo[b], ACT.Identity, scale=f[:, 0, 1 - n:2 - n],
                                     bias=f[:, 1, 1 - n:2 - n]).then_inc(s_nrm, 1)

            def pair_columns(slot, j):
                act.drain()
                nc.scalar.copy(pair_tab[:, slot, 0, :], rstd[:, :, ds(j, 1)].rearrange("p n a -> p (n a)"))
                nc.scalar.copy(pair_tab[:, slot, 1, :], nmr[:, :, ds(j, 1)].rearrange("p n a -> p (n a)"))
                act.drain()

            with act.Fori(0, D_STEPS) as i:
                pair_columns(0, i)
                for t in range(TILES_D):
                    T, j, n = tile_of(i, t)
                    if n == 0:
                        pair_columns(1, j)
                    e0, e1, f0, f1, f2, f3 = per_tile[t]

                    nj, nn = next_of(j, n)
                    for q in range(2):
                        act.wait_ge(s_tp, PX + 4 * (T + 1) + q - 1)
                        act.dma_start(xc[:, q, :], xr[rows(nn, nj), cols(q)]).then_inc(s_xc[q], 16)

                    def norms(group):
                        for k in group:
                            norm_unit(i, k)

                    norms(e0)
                    hi_part(T + 1, 1 - n, 0, PX)
                    norms(e1)
                    hi_part(T + 1, 1 - n, 1, PX)
                    hwT_out(T)
                    norms(f0)
                    silu(T, 0)
                    silu(T, 1)
                    hi_part(T + 1, 1 - n, 2, PX)
                    norms(f1)
                    hi_part(T + 1, 1 - n, 3, PX)
                    silu(T, 2)
                    norms(f2)
                    silu(T, 3)
                    norms(f3)

        @block.vector
        def _(dve):
            v = nc.vector

            def row_stats(src):
                for n in range(2):
                    for q in range(NQ):
                        v.bn_stats(bn[:, n, q, :], src[n][:, cols(q)])
                dve.drain()
                for n in range(2):
                    v.bn_aggr(mv[:, n, :], bn[:, n, :, :])
                dve.drain()
                v.tensor_scalar(vare[:, :], mv[:, :, 1], EPS, None, ALU.add).then_inc(s_var, 1)

            def row_tables(j, count):
                dve.wait_ge(s_std, count)
                v.reciprocal(r2[:, :], std[:, :])
                dve.drain()
                v.scalar_tensor_tensor(out=std[:, :], in0=mv[:, :, 0], scalar=-1.0, in1=r2[:, :],
                                       op0=ALU.mult, op1=ALU.mult)
                v.tensor_copy(mean[:, :, ds(j, 1)].rearrange("p n a -> p (n a)"), mv[:, :, 0])
                v.tensor_scalar(rs[:, :, ds(j, 1)].rearrange("p n a -> p (n a)"), r2[:, :], XS, None, ALU.mult)
                v.tensor_copy(rstd[:, :, ds(j, 1)].rearrange("p n a -> p (n a)"), r2[:, :])
                dve.drain()
                v.tensor_copy(nmr[:, :, ds(j, 1)].rearrange("p n a -> p (n a)"), std[:, :]).then_inc(s_rstd, 1)

            dve.wait_ge(s_x0, 32)
            row_stats([stage[2], stage[3]])
            dve.wait_ge(s_ident, IDENT)
            row_tables(0, 1)

            def scale_item(m):
                np_ = E if m == IT_R else P
                one = slice(m, m + 1)
                dve.wait_ge(s_l1, (m if m < IT_A else m - 1) + 1)
                v.tensor_scalar(l1[0:np_, one], l1[0:np_, one], 2.0 ** -100, None, ALU.max)
                dve.drain()
                v.tensor_scalar(eb[0:np_, one], l1[0:np_, one].bitcast(U32), 0xFF * EXP, None, ALU.bitwise_and)
                dve.drain()
                v.tensor_scalar(sc[0:np_, one], eb[0:np_, one], -1.0, float((2 * 127 + 14) * EXP), ALU.mult, ALU.add)
                v.tensor_scalar(us[0:np_, one], eb[0:np_, one], float(-(14 + 8) * EXP), None, ALU.add)
                dve.drain()
                v.tensor_scalar(isc[0:np_, one], sc[0:np_, one].bitcast(F32), XS, None, ALU.mult)
                v.tensor_scalar(stage[m % 4][0:np_, :], stage[m % 4][0:np_, :], sc[0:np_, one].bitcast(F32), None,
                                ALU.mult).then_inc(s_scaled, 1)

            scale_item(0)
            hi_seen = 0
            for m in range(ITEMS):
                if m + 1 < IT_A:
                    scale_item(m + 1)
                elif m + 1 == IT_A:
                    dve.wait_ge(s_item[IT_A % 4], 16 * (IT_A // 4 + 1))
                    dve.wait_ge(s_itdone, WT)
                    v.tensor_copy(a_grouped.rearrange("p (k e r) -> p k e r", k=KB, e=E),
                                  stage[IT_A % 4].rearrange("p (e k r) -> p k e r", e=E, k=KB)).then_inc(s_scaled, 1)
                if m == IT_R:
                    hi_seen += 1
                    dve.wait_ge(s_whi, hi_seen)
                    v.tensor_tensor(a_lo[:, :, ER:AUG], hb[:, 0:P].rearrange("p (k e) -> p k e", e=E),
                                    a_hi[:, :, ER:AUG], ALU.subtract).then_inc(s_augu, 1)
                elif m == IT_A:
                    at = stage[IT_AT % 4].rearrange("a (p k) -> a k p", k=KB)
                    dve.wait_ge(s_itdone, IT_AT - 3)
                    for q in range(4):
                        g = group_of(m) + q
                        dve.wait_ge(s_wtp, g + 1)
                        v.tensor_copy(at[:, 4 * q:4 * q + 4, :],
                                      zb[g % 4][:, :].rearrange("p (k o) -> p k o", k=4)).then_inc(s_zused, 1)
                    dve.drain()
                    v.memset(sp_n[:, :], 0.0).then_inc(s_at, 1)
                    scale_item(IT_AT)
                else:
                    for q in range(4):
                        g = group_of(m) + q
                        hi_seen += 1
                        dve.wait_ge(s_whi, hi_seen)
                        v.tensor_tensor(w_dst((w_lo, a_lo), m, q), zb[g % 4][:, :].rearrange("p (k o) -> p k o", k=4),
                                        w_dst((w_hi, a_hi), m, q), ALU.subtract).then_inc(s_zused, 1)

            def build_diag(slot, columns, built):
                if built >= 2:
                    dve.wait_ge(s_zused, W_GROUPS + built - 1)
                for a, (col, np_) in enumerate(columns):
                    v.tensor_scalar(slot[0:np_, a * P:a * P + np_], ident[0:np_, 0:np_], col, None, ALU.mult)
                dve.drain()
                v.memset(sp_n[:, :], 0.0).then_inc(s_diag, 1)

            def read_row(r):
                dve.wait_ge(s_wtp, W_GROUPS + r + 1)
                if r < 4:
                    v.tensor_copy(unscale[:, cols(r)], zb[r][:, :]).then_inc(s_zused, 1)
                else:
                    v.tensor_tensor(b_lora[:, cols(r - 4)], b_lora[:, cols(r - 4)], zb[r - 4][:, :], ALU.mult)\
                        .then_inc(s_zused, 1)

            dve.drain()
            dve.wait_ge(s_const, 48)
            for r in range(8):
                table = us[:, :].bitcast(F32) if r < 4 else isc[:, :]
                build_diag(diag[r % 2], [(table[:, 4 * (r % 4) + a:4 * (r % 4) + a + 1], P) for a in range(4)], r)
                if r:
                    read_row(r - 1)
            read_row(7)
            build_diag(diag[0], [(us[:, IT_AT:IT_AT + 1].bitcast(F32), P), (us[0:E, IT_R:IT_R + 1].bitcast(F32), E)], 0)
            dve.wait_ge(s_aug, 2)
            v.tensor_copy(unscale_aug[:, :], hb[:, 0:AUG]).then_inc(s_augu, 1)

            def norm_chunk(T, j, n, q):
                dve.wait_ge(s_xc[q % 2], 16 * (2 * T + q // 2 + 1))
                v.tensor_scalar(xc[:, q % 2, :], xc[:, q % 2, :], mean[:, n, ds(j, 1)], rs[:, n, ds(j, 1)],
                                ALU.subtract, ALU.mult).then_inc(s_xn, 1)

            def lo_part(T, n, q):
                dve.wait_ge(s_hi, 4 * T + q + 1)
                v.tensor_tensor(xt_lo[:, n, 4 * q:4 * q + 4, :], tp[q % 2][:, :].rearrange("p (k r) -> p k r", k=4),
                                xt_hi[:, n, 4 * q:4 * q + 4, :], ALU.subtract).then_inc(s_lo, 1)

            dve.drain()
            norm_chunk(0, 0, 0, 0)
            norm_chunk(0, 0, 0, 1)
            for q in range(4):
                lo_part(0, 0, q)
                if q < 2:
                    norm_chunk(0, 0, 0, q + 2)

            def mix_h(T):
                dve.wait_ge(s_h, T + 1)
                dve.wait_ge(s_hwtp, AHEAD + T)
                v.tensor_tensor(haug[:, :], hb[:, 0:AUG], unscale_aug[:, :], ALU.mult)
                dve.drain()
                v.tensor_tensor(sp_z[:, :], haug[:, ER:AUG], bias_r[:, :], ALU.add)
                dve.drain()
                v.max(sp_s[:, :], sp_z[:, :])
                dve.drain()
                v.tensor_tensor_scan(sp_c[:, :], one8[:, :], sp_s[:, :], 0.0, ALU.mult, ALU.add)
                v.tensor_tensor(sp_k[:, :], sp_s[:, :], kio[:, :], ALU.mult)
                dve.drain()
                v.scalar_tensor_tensor(out=sp_u[:, :], in0=sp_k[:, :], scalar=1.0, in1=sp_c[:, :],
                                       op0=ALU.add, op1=ALU.is_gt, accum_out=sp_n[:, 0:1])
                dve.drain()
                v.scalar_tensor_tensor(out=sp_v[:, :], in0=sp_s[:, :], scalar=1.0, in1=sp_u[:, :],
                                       op0=ALU.mult, op1=ALU.mult, accum_out=sp_n[:, 1:2])
                v.reciprocal(sp_n[:, 2:3], sp_n[:, 0:1])
                dve.drain()
                v.tensor_scalar(sp_n[:, 3:4], sp_n[:, 1:2], -1.0, sp_n[:, 2:3], ALU.add, ALU.mult)
                dve.drain()
                v.tensor_scalar(sp_w[:, :], sp_z[:, :], sp_n[:, 3:4], 0.0, ALU.subtract, ALU.max)
                dve.drain()
                v.tensor_tensor(hw[:, :].rearrange("p (e r) -> p e r", e=E),
                                haug[:, 0:ER].rearrange("p (e r) -> p e r", e=E),
                                sp_w[:, :].rearrange("p (e a) -> p e a", a=1).to_broadcast([P, E, R]),
                                ALU.mult).then_inc(s_hw, 1)

            def z_out(T, qs):
                for q in qs:
                    dve.wait_ge(s_z, AHEAD + 4 * T + q + 1)
                    v.tensor_tensor(zs[:, q % 2, :], zb[q][:, :], unscale[:, cols(q)], ALU.mult).then_inc(s_zused, 1)
                dve.drain()
                for q in qs:
                    v.tensor_tensor(zs[:, q % 2, :], zs[:, q % 2, :], bias[:, cols(q)], ALU.add).then_inc(s_zb, 1)

            def g_stored(T, q):
                dve.wait_ge(s_gst[q % 2], AHEAD + 16 * (2 * T + q // 2))

            v.memset(acc[0], 0.0)
            v.memset(acc[1], 0.0)
            dve.drain()

            def pair_stats(p):
                dve.wait_ge(s_xp, 32 * p + 32)
                row_stats(xp)
                row_tables(p, p + 2)

            def pair_sums(p, half):
                part = slice(half * 1024, half * 1024 + 1024)
                if half == 0:
                    dve.wait_ge(s_xnp, 2 * p + 2)
                v.tensor_tensor(dtmp, xp[1][:, part], xp[0][:, part], ALU.subtract)
                dve.drain()
                v.tensor_tensor(xp[0][:, part], xp[0][:, part], dtmp, ALU.mult)
                v.tensor_tensor(xp[1][:, part], xp[1][:, part], dtmp, ALU.mult)
                dve.drain()
                v.tensor_tensor(acc[0][:, part], acc[0][:, part], xp[0][:, part], ALU.add)
                last = v.tensor_tensor(acc[1][:, part], acc[1][:, part], xp[1][:, part], ALU.subtract)
                if half == 1:
                    dve.drain()
                    v.memset(sp_v[:, :], 0.0).then_inc(s_acc, 1)

            with dve.Fori(0, B_PAIRS) as i:
                for n in range(2):
                    T = 2 * i + n
                    nj, nn = next_of(i, n)
                    p = B_STATS * i + n
                    mix_h(T)
                    pair_stats(p)
                    norm_chunk(T + 1, nj, nn, 0)
                    norm_chunk(T + 1, nj, nn, 1)
                    pair_sums(p, 0)
                    lo_part(T + 1, nn, 0)
                    norm_chunk(T + 1, nj, nn, 2)
                    pair_sums(p, 1)
                    lo_part(T + 1, nn, 1)
                    norm_chunk(T + 1, nj, nn, 3)
                    lo_part(T + 1, nn, 2)
                    g_stored(T, 0)
                    g_stored(T, 1)
                    z_out(T, (0, 1))
                    lo_part(T + 1, nn, 3)
                    g_stored(T, 2)
                    z_out(T, (2,))
                    g_stored(T, 3)
                    z_out(T, (3,))

            dve.wait_ge(s_dsum, 1)
            v.tensor_scalar(dcol[:, :], hb[:, 0:2 * KB], float(C) ** -0.5, None, ALU.mult)
            dve.drain()
            v.tensor_scalar(ex[:, 0:2 * KB], dcol[:, :], 0.0, -1.0, ALU.max, ALU.mult)
            dve.drain()
            v.tensor_tensor(ex[:, 2 * KB:4 * KB], dcol[:, :], ex[:, 0:2 * KB], ALU.add).then_inc(s_d, 1)
            dve.wait_ge(s_e, 1)
            v.tensor_tensor(dcol[:, :], ex[:, 0:2 * KB], ex[:, 2 * KB:4 * KB], ALU.add)
            dve.drain()
            v.reciprocal(dcol[:, :], dcol[:, :])
            dve.drain()
            v.tensor_tensor(dcol[:, :], dcol[:, :], ex[:, 2 * KB:4 * KB], ALU.mult)
            dve.drain()

            def p_row(g):
                dve.wait_ge(s_tp, 4 * (B_TILES + 1) + g + 1)
                v.tensor_copy(prow[g // NQ][:, cols(g % NQ)], tp[g % 2][:, :]).then_inc(s_lo, 1)

            for g in range(2 * NQ):
                if g >= 2:
                    p_row(g - 2)
                for a in range(BPQ):
                    v.tensor_scalar(diag[g % 2][:, a * P:(a + 1) * P], ident[:, :],
                                    dcol[:, BPQ * g + a:BPQ * g + a + 1], None, ALU.mult)
                dve.drain()
                v.memset(sp_n[:, :], 0.0).then_inc(s_diag, 1)
            p_row(2 * NQ - 2)
            p_row(2 * NQ - 1)
            dve.drain()
            v.memset(sp_n[:, :], 0.0).then_inc(s_fin, fin0)
            dve.drain()

            def finish(i, k):
                kind, _t, _q = units[k]
                n, j, q, T = unit_place(i, units[k])
                b = k % 2
                dve.wait_ge(s_nrm, UNITS * i + k + 1)
                v.tensor_tensor(xo[b], xo[b], na[b], ALU.subtract)
                dve.drain()
                v.tensor_tensor(xo[b], xo[b], prow[n][:, cols(q)], ALU.mult)
                dve.drain()
                v.scalar_tensor_tensor(out=na[b], in0=na[b], scalar=2.0, in1=xo[b], op0=ALU.mult, op1=ALU.add)
                dve.drain()
                if kind == "tile":
                    dve.wait_ge(s_g, 4 * T + q + 1)
                v.tensor_tensor(na[b], na[b], gx[b] if kind == "early" else zs[:, q % 2, :], ALU.mult)
                dve.drain()
                v.tensor_tensor(na[b], na[b], xa[b], ALU.add).then_inc(s_fin, 1)

            with dve.Fori(0, D_STEPS) as i:
                for t in range(TILES_D):
                    T, j, n = tile_of(i, t)
                    nj, nn = next_of(j, n)
                    e0, e1, f0, f1, f2, f3 = per_tile[t]

                    def finishes(group):
                        for k in group:
                            finish(i, k)

                    mix_h(T)
                    norm_chunk(T + 1, nj, nn, 0)
                    norm_chunk(T + 1, nj, nn, 1)
                    finishes(e0)
                    lo_part(T + 1, nn, 0)
                    norm_chunk(T + 1, nj, nn, 2)
                    finishes(e1)
                    lo_part(T + 1, nn, 1)
                    norm_chunk(T + 1, nj, nn, 3)
                    z_out(T, (0, 1))
                    finishes(f0)
                    lo_part(T + 1, nn, 2)
                    finishes(f1)
                    lo_part(T + 1, nn, 3)
                    z_out(T, (2,))
                    finishes(f2)
                    z_out(T, (3,))
                    finishes(f3)

        @block.tensor
        def _(pe):
            mm = nc.tensor.matmul

            pe.wait_ge(s_ident, IDENT)
            for m in range(ITEMS):
                pe.wait_ge(s_scaled, m + 1)
                if m == IT_R:
                    for k in range(KB):
                        last = nc.tensor.transpose(hb[:, k * E:(k + 1) * E], stage[m % 4][0:E, k * P:(k + 1) * P],
                                                   ident[0:E, 0:E])
                    last.then_inc(s_aug, 1)
                else:
                    for q in range(4):
                        g = group_of(m) + q
                        if g >= 4:
                            pe.wait_ge(s_zused, g - 3)
                        for a in range(4):
                            k = 4 * q + a
                            src = (a_grouped if m == IT_A else stage[m % 4])[:, k * P:(k + 1) * P]
                            last = nc.tensor.transpose(zb[g % 4][:, a * P:(a + 1) * P], src, ident[:, :])
                        last.then_inc(s_wtp, 1)
                pe.drain()
                nc.tensor.nop().then_inc(s_itdone, 1)
            for r in range(8):
                pe.wait_ge(s_diag, r + 1)
                pe.wait_ge(s_zused, W_GROUPS + r - 3)
                mm(zb[r % 4][:, :], ones[:, :], diag[r % 2], start=True, stop=True).then_inc(s_wtp, 1)
            pe.wait_ge(s_diag, 9)
            pe.wait_ge(s_augu, 1)
            mm(hb[:, 0:ER], ones[:, :], diag[0][:, 0:ER], start=True, stop=True)
            mm(hb[:, ER:AUG], ones[0:E, :], diag[0][0:E, P:P + E], start=True, stop=True).then_inc(s_aug, 1)

            def transpose_chunk(T, q, px):
                pe.wait_ge(s_xn, 4 * T + q + 1)
                if not (isinstance(T, int) and 4 * T + q < 2):
                    pe.wait_ge(s_lo, px + 4 * T + q - 1)
                for a in range(4):
                    last = nc.tensor.transpose(tp[q % 2][:, a * P:(a + 1) * P], xc[:, q % 2, a * P:(a + 1) * P],
                                               ident[:, :])
                last.then_inc(s_tp, 1)

            def passes(n, k):
                return ((xt_hi[:, n, k, :], 0), (xt_hi[:, n, k, :], 1), (xt_lo[:, n, k, :], 0))

            def base(T, n, c, ks):
                if ks[0] == 0:
                    pe.wait_ge(s_zused, ZG + 4 * T + c - 3)
                for k in ks:
                    for a, (lhs, w) in enumerate(passes(n, k)):
                        mm(zb[c][:, :], lhs, (w_hi, w_lo)[w][:, k, cols(c)], start=(k == 0 and a == 0), stop=False)

            def lora(T, c):
                mm(zb[c][:, :], hwT[:, :], b_lora[:, cols(c)], start=False, stop=True).then_inc(s_z, 1)

            def tile(T, n, px):
                pe.wait_ge(s_lo, px + 4 * T + 4)
                pe.wait_ge(s_hw, AHEAD + T)
                for k in range(KB):
                    for a, (lhs, w) in enumerate(passes(n, k)):
                        last = mm(hb[:, 0:AUG], lhs, (a_hi, a_lo)[w][:, k, :], start=(k == 0 and a == 0),
                                  stop=(k == KB - 1 and a == 2))
                last.then_inc(s_h, 1)
                base(T, n, 0, range(KB))
                transpose_chunk(T + 1, 0, px)
                base(T, n, 1, range(KB))
                transpose_chunk(T + 1, 1, px)
                pe.wait_ge(s_hw, AHEAD + T + 1)
                pe.wait_ge(s_hwT, AHEAD + T)
                nc.tensor.transpose(hwb[0:ER, 0:P], hw[:, :], ident[:, :]).then_inc(s_hwtp, 1)
                base(T, n, 2, range(0, HALF))
                transpose_chunk(T + 1, 2, px)
                pe.wait_ge(s_hwT, AHEAD + T + 1)
                lora(T, 0)
                lora(T, 1)
                base(T, n, 2, range(HALF, KB))
                lora(T, 2)
                transpose_chunk(T + 1, 3, px)
                base(T, n, 3, range(KB))
                lora(T, 3)

            for q in range(4):
                transpose_chunk(0, q, 0)
            pe.wait_ge(s_augu, 2)
            with pe.Fori(0, B_PAIRS) as i:
                for n in range(2):
                    tile(2 * i + n, n, 0)
            pe.wait_ge(s_acc, AHEAD + PAIRS)
            pe.wait_ge(s_hw, AHEAD + B_TILES)
            for k in range(2 * KB):
                last = mm(hb[:, k:k + 1], acc[k // KB][:, (k % KB) * P:(k % KB + 1) * P], ones[:, 0:1],
                          start=True, stop=True)
            last.then_inc(s_dsum, 1)
            for g in range(2 * NQ):
                pe.wait_ge(s_diag, 9 + g + 1)
                pe.wait_ge(s_lo, 4 * (B_TILES + 1) + g - 1)
                mm(tp[g % 2][:, :], ones[:, :], diag[g % 2], start=True, stop=True).then_inc(s_tp, 1)
            with pe.Fori(0, D_STEPS) as i:
                for t in range(TILES_D):
                    T, _j, n = tile_of(i, t)
                    tile(T, n, PX)


def kernel(L0_attn_x, L0_ffn_W_base, L0_ffn_b_base, L0_ffn_W_router, L0_ffn_b_router, L0_ffn_lora_A, L0_ffn_lora_B):
    import numpy as np
    import concourse.bacc as bacc
    from concourse import mybir
    from concourse.bass_utils import run_bass_kernel_spmd

    nc = bacc.Bacc("TRN2", target_bir_lowering=False, num_devices=1, dynamic_dma_scratch_size=1024)
    ins = {
        "in_x": L0_attn_x, "in_w_base": L0_ffn_W_base, "in_b_base": L0_ffn_b_base, "in_w_router": L0_ffn_W_router,
        "in_b_router": L0_ffn_b_router, "in_lora_a": L0_ffn_lora_A, "in_lora_b": L0_ffn_lora_B,
    }
    ins = {k: np.ascontiguousarray(a) for k, a in ins.items()}
    args = [nc.dram_tensor(k, a.shape, mybir.dt.from_np(a.dtype), kind="ExternalInput").ap() for k, a in ins.items()]
    shape = ins["in_x"].shape
    out = nc.dram_tensor("out_0", shape, mybir.dt.float32, kind="ExternalOutput").ap()
    g_dram = nc.dram_tensor("g_early", (shape[1], shape[2]), mybir.dt.float32, kind="Internal").ap()
    build(nc, *args, out, g_dram)
    r = run_bass_kernel_spmd(nc, [ins], core_ids=[0])
    return r.results[0]["out_0"]
```

```python
def build(nc, x, W, b_base, Wr, b_router, lora_A, lora_B, out, g_dram):
    from contextlib import ExitStack

    import concourse.bass as bass
    from concourse import mybir

    F32, F16, BF16, U32 = mybir.dt.float32, mybir.dt.float16, mybir.dt.bfloat16, mybir.dt.uint32
    ALU = mybir.AluOpType
    ACT = mybir.ActivationFunctionType
    AX = mybir.AxisListType
    ds = bass.ds

    P = 128
    _, C, L = x.shape
    O = W.shape[0]
    E, _, R = lora_A.shape
    ER = E * R
    KB = L // P
    CH = 512
    NQ = L // CH
    BPQ = CH // P
    HALF = KB // 2
    PAIRS = C // P
    AUG = ER + E
    XS = 2.0 ** 8
    EPS = 1e-5
    H_UNSCALE = 2.0 ** -13
    AHEAD = 1
    EXP = 1 << 23

    B_PAIRS = 8
    B_STATS = PAIRS // B_PAIRS
    D_STEPS = B_PAIRS
    D_PAIRS = (PAIRS - B_PAIRS) // D_STEPS
    B_TILES = 2 * B_PAIRS

    WT = O // P
    IT_A, IT_R, IT_AT, IT_W = 0, 1, 2, 3
    ITEMS = IT_W + WT

    G_X0 = 0
    G_A = G_X0 + 4
    G_X1 = G_A + 4
    G_AT = G_X1 + 4
    G_W = G_AT + 4
    G_X2 = G_W + 4 * WT
    TB = G_X2 - 4 * 2
    HB = TB - 4
    WIDE = G_W + 4 * 8
    PX = 8

    xr = x.rearrange("b c l -> (b c) l")
    outr = out.rearrange("b c l -> (b c) l")

    with ExitStack() as ctx:
        def sb(name, shape, dt):
            return ctx.enter_context(nc.sbuf_tensor(name, shape, dt))

        def sem(name):
            return ctx.enter_context(nc.semaphore(name))

        w_hi = sb("w_hi", [P, KB, O], F16)
        w_lo = sb("w_lo", [P, KB, O], F16)
        a_hi = sb("a_hi", [P, KB, AUG], F16)
        a_lo = sb("a_lo", [P, KB, AUG], F16)
        b_lora = sb("b_lora", [ER, NQ, 2, CH], F16)
        unscale = sb("unscale", [P, O], BF16)
        bias = sb("bias", [P, O], F32)
        unscale_aug = sb("unscale_aug", [P, AUG], F32)
        bias_r = sb("bias_r", [P, E], F32)
        xt_hi = sb("xt_hi", [P, 2, KB, P], F16)
        xt_lo = sb("xt_lo", [P, 2, KB, P], F16)
        xc = sb("xc", [P, 2, CH], F32)
        zs = sb("zs", [P, 2, CH], F32)
        ident = sb("ident", [P, P], F32)
        mean = sb("mean", [P, 2, PAIRS + 1], F32)
        rs = sb("rs", [P, 2, PAIRS + 1], F32)
        rstd = sb("rstd", [P, 2, PAIRS + 1], F32)
        nmr = sb("nmr", [P, 2, PAIRS + 1], F32)
        pair_tab = sb("pair_tab", [P, 2, 2, 2], F32)
        bn = sb("bn", [P, 2, NQ, 6], F32)
        mv = sb("mv", [P, 2, 2], F32)
        vare = sb("vare", [P, 2], F32)
        std = sb("std", [P, 2], F32)
        r2 = sb("r2", [P, 2], F32)
        l1 = sb("l1", [P, 2, ITEMS], F32)
        eb = sb("eb", [P, ITEMS], U32)
        sc = sb("sc", [P, ITEMS], U32)
        us = sb("us", [P, ITEMS], U32)
        isc = sb("isc", [P, ITEMS], F32)
        kio = sb("kio", [P, E], F32)
        one8 = sb("one8", [P, E], F32)
        haug = sb("haug", [P, AUG], F32)
        dcol = sb("dcol", [P, 2 * KB], F32)
        ex = sb("ex", [P, 4 * KB], F32)
        hw = sb("hw", [P, ER], F32)
        hwT = sb("hwT", [ER, 2, 2, P], F16)
        l1_at = sb("l1_at", [P, 1], BF16)
        extra = sb("extra", [P, WT], F32)
        sp_z = sb("sp_z", [P, E], F32)
        sp_s = sb("sp_s", [P, E], F32)
        sp_c = sb("sp_c", [P, E], F32)
        sp_k = sb("sp_k", [P, E], F32)
        sp_u = sb("sp_u", [P, E], F32)
        sp_v = sb("sp_v", [P, E], F32)
        sp_w = sb("sp_w", [P, E], F32)
        sp_n = sb("sp_n", [P, 4], F32)

        work = sb("work", [P, 4 * L + 1024], F32)
        stage = [work[:, (2 + k) % 4 * L:((2 + k) % 4 + 1) * L] for k in range(4)]
        a_grouped, *raw0 = [w_hi[:, 2 * k:2 * k + 2, :].rearrange("p k o -> p (k o)").bitcast(F32) for k in range(3)]
        abs_b = w_hi[:, 6, :].bitcast(BF16)
        raw_b = b_lora.rearrange("p c h o -> p (c h o)").bitcast(F32)
        diag = [work[:, 4 * L + k * CH:4 * L + (k + 1) * CH] for k in range(2)]
        diag_row = [d[:, 0:CH // 2].bitcast(BF16) for d in diag]
        acc = [work[:, n * L:(n + 1) * L] for n in range(2)]
        xp = [work[:, (2 + n) * L:(3 + n) * L] for n in range(2)]
        dtmp = work[:, 4 * L:4 * L + 1024]
        prow = xp
        xa = [work[:, k * CH:(k + 1) * CH] for k in range(2)]
        xo = [work[:, (2 + k) * CH:(3 + k) * CH] for k in range(2)]
        na = [work[:, (4 + k) * CH:(5 + k) * CH] for k in range(2)]
        gx = [work[:, (6 + k) * CH:(7 + k) * CH] for k in range(2)]
        ones = sb("ones", [P, P], F32)
        ones_row = sb("ones_row", [P, P], BF16)

        zb = [ctx.enter_context(nc.psum_tensor(f"zb{k}", [P, CH], F32)) for k in range(4)]
        tp = [ctx.enter_context(nc.psum_tensor(f"tp{k}", [P, CH], F32)) for k in range(2)]

        def tp_bank(q, group):
            wide = isinstance(group, int) and group < WIDE
            return (tp[0], tp[1], zb[2], zb[3])[q] if wide else tp[q % 2]

        hb = ctx.enter_context(nc.psum_tensor("hb", [P, CH], F32))
        hwb = ctx.enter_context(nc.psum_tensor("hwb", [P, CH], F32))

        def row_bank(c, k):
            return hwb if k == 0 or c == 0 else hb

        dsum = hwb[:, P:P + 2 * KB]

        s_const = sem("s_const")
        s_bias_r = sem("s_bias_r")
        s_bias = sem("s_bias")
        s_absb = sem("s_absb")
        s_bound = sem("s_bound")
        s_ident = sem("s_ident")
        s_x0 = sem("s_x0")
        s_item = [sem(f"s_item{k}") for k in range(4)]
        s_ag = sem("s_ag")
        s_l1 = sem("s_l1")
        s_scaled = sem("s_scaled")
        s_at = sem("s_at")
        s_diag = sem("s_diag")
        s_zused = sem("s_zused")
        s_rt = sem("s_rt")
        s_rhi = sem("s_rhi")
        s_row = sem("s_row")
        s_rowu = sem("s_rowu")
        s_var = sem("s_var")
        s_std = sem("s_std")
        s_rstd = sem("s_rstd")
        s_xc = [sem(f"s_xc{k}") for k in range(2)]
        s_xn = sem("s_xn")
        s_tp = sem("s_tp")
        s_hi = sem("s_hi")
        s_lo = sem("s_lo")
        s_h = sem("s_h")
        s_hw = sem("s_hw")
        s_hwtp = sem("s_hwtp")
        s_hwT = sem("s_hwT")
        s_hwl = sem("s_hwl")
        s_z = sem("s_z")
        s_zb = sem("s_zb")
        s_g = sem("s_g")
        s_gst = [sem(f"s_gst{k}") for k in range(2)]
        s_xp = sem("s_xp")
        s_xnp = sem("s_xnp")
        s_acc0 = sem("s_acc0")
        s_acc = sem("s_acc")
        s_dsum = sem("s_dsum")
        s_d = sem("s_d")
        s_e = sem("s_e")
        s_fin = sem("s_fin")
        s_fl = [sem(f"s_fl{k}") for k in range(2)]
        s_nrm = sem("s_nrm")
        s_out = [sem(f"s_out{k}") for k in range(2)]

        TILES_D = 2 * D_PAIRS
        early = [("early", n, q) for n in range(2) for q in range(NQ)]
        units, per_tile = [], {}
        for t in range(TILES_D):
            share = [early.pop(0) for _ in range(2 * NQ // TILES_D)]
            per_tile[t] = []
            for group in (share[0:2], share[2:4], [("tile", t, 0)], [("tile", t, 1)], share[4:] + [("tile", t, 2)],
                          [("tile", t, 3)]):
                per_tile[t].append(range(len(units), len(units) + len(group)))
                units += group
        assert not early and len(units) == TILES_D * NQ + 2 * NQ
        UNITS = len(units)
        load_count, total = [], [0, 0]
        for k, u in enumerate(units):
            total[k % 2] += 48 if u[0] == "early" else 32
            load_count.append(total[k % 2])
        fin0 = 2

        def tile_of(i, t):
            return B_TILES + TILES_D * i + t, B_PAIRS + D_PAIRS * i + t // 2, t % 2

        def next_of(j, n):
            return (j, 1) if n == 0 else (j + 1, 0)

        def rows(n, j):
            return ds(j * P + n * C, P)

        def cols(q):
            return slice(q * CH, (q + 1) * CH)

        def unit_place(i, u):
            kind, t, q = u
            if kind == "early":
                return t, i, q, None
            T, j, n = tile_of(i, t)
            return n, j, q, T

        block = ctx.enter_context(nc.Block())

        @block.sync
        def _(sp):
            sp.dma_start(stage[IT_R][0:E, :], Wr).then_inc(s_item[IT_R], 16)
            for n in range(2):
                sp.dma_start(raw0[n], xr[rows(n, 0), :]).then_inc(s_x0, 16)
            sp.dma_start(stage[IT_A].rearrange("p (e v) -> p e v", e=E),
                         lora_A.rearrange("e (p k) r -> p e (k r)", p=P)).then_inc(s_item[IT_A], 16)

            def load_chunk(T, j, n, q, group=None):
                if group is not None:
                    sp.wait_ge(s_tp, group + 1)
                sp.dma_start(xc[:, q % 2, :], xr[rows(n, j), cols(q)]).then_inc(s_xc[q % 2], 16)

            def load_w(m):
                k = (IT_W + m) % 4
                sp.dma_start(stage[k], W[m * P:(m + 1) * P, :]).then_inc(s_item[k], 16)

            load_w(0)
            sp.dma_start(raw_b, lora_B.rearrange("e r o -> (e r) o")).then_inc(s_const, 16)
            sp.wait_ge(s_ag, 1)
            load_w(1)
            sp.wait_ge(s_rt, 1)
            load_w(2)
            sp.dma_start(bias_r[:, :], b_router.rearrange("(a e) -> a e", a=1).to_broadcast([P, E]))\
                .then_inc(s_bias_r, 16)
            for m in range(3, WT):
                sp.wait_ge(s_tp, G_AT + 4 * (m - 2))
                load_w(m)
                if m == 4:
                    sp.dma_start(bias[:, :], b_base.rearrange("(a o) -> a o", a=1).to_broadcast([P, O]))\
                        .then_inc(s_bias, 16)
                    for q in range(2):
                        load_chunk(2, 1, 0, q)

            def load_pair(p, order):
                sp.wait_ge(s_acc, AHEAD + order)
                for n in range(2):
                    sp.dma_start(xp[n], xr[rows(n, p), :]).then_inc(s_xp, 16)

            for n in range(2):
                sp.wait_ge(s_tp, G_X2 - 4 * (2 - n))
                sp.dma_start(xp[n], xr[rows(n, 1), :]).then_inc(s_xp, 16)
            load_chunk(2, 1, 0, 2, G_X2)
            load_chunk(2, 1, 0, 3, G_X2 + 1)

            def load_rest(T, i, n, qs=(2, 3)):
                nj, nn = next_of(i, n)
                for q in qs:
                    load_chunk(T + 1, nj, nn, q, TB + 4 * (T + 1) + q - 2)

            def load_ahead(T, j, n):
                for q in range(2):
                    load_chunk(T + 2, j, n, q, TB + 4 * (T + 1) + q + 2)

            for q in range(2):
                load_chunk(3, 1, 1, q, G_X2 + q + 2)

            def early_pair(i, first=False):
                for n in range(2):
                    T = 2 * i + n
                    if first and n == 0:
                        load_pair(0, 1)
                        load_rest(T, i, n)
                        load_pair(2, 2)
                    elif first:
                        load_rest(T, i, n, (2,))
                        load_pair(3, 3)
                        load_rest(T, i, n, (3,))
                    else:
                        load_pair(B_STATS * i + n, B_STATS * i + n)
                        load_rest(T, i, n)
                    load_ahead(T, i + 1, n)

            early_pair(1, first=True)
            with sp.Fori(2, B_PAIRS) as i:
                early_pair(i)

            for k in range(2):
                sp.wait_ge(s_gst[k], AHEAD + 16 * B_TILES * 2)

            def load_unit(i, k, ahead=0):
                n, j, q, _ = unit_place(i, units[k])
                b = k % 2
                down = ahead * P
                sp.dma_start(xa[b], xr[down:, :][rows(n, j), cols(q)]).then_inc(s_fl[b], 16)
                sp.dma_start(xo[b], xr[down:, :][rows(1 - n, j), cols(q)]).then_inc(s_fl[b], 16)
                if units[k][0] == "early":
                    sp.dma_start(gx[b], g_dram[down:, :][ds(j * P + n * B_PAIRS * P, P), cols(q)])\
                        .then_inc(s_fl[b], 16)

            def store_unit(i, k, last):
                n, j, q, _ = unit_place(i, units[k])
                sp.wait_ge(s_fin, fin0 + UNITS * i + k + 1)
                sp.dma_start(outr[rows(n, j), cols(q)], na[k % 2]).then_inc(s_out[k % 2], 16)
                if k + 2 < UNITS:
                    load_unit(i, k + 2)
                elif not last:
                    load_unit(i, k + 2 - UNITS, 1)

            sp.wait_ge(s_fin, fin0)
            load_unit(0, 0)
            load_unit(0, 1)
            def final_step(i, last=False):
                for t in range(TILES_D):
                    T, j, n = tile_of(i, t)
                    nj, nn = next_of(j, n)
                    e0, e1, f0, f1, f2, f3 = per_tile[t]

                    def load_next(q):
                        if last and t == TILES_D - 1:
                            return
                        sp.wait_ge(s_tp, TB + PX + 4 * (T + 1) + q - 1)
                        sp.dma_start(xc[:, q % 2, :], xr[rows(nn, nj), cols(q)]).then_inc(s_xc[q % 2], 16)

                    load_next(2)
                    for k in e0:
                        store_unit(i, k, last)
                    load_next(3)
                    for k in e1:
                        store_unit(i, k, last)
                    for group in (f0, f1, f2, f3):
                        for k in group:
                            store_unit(i, k, last)

            with sp.Fori(0, D_STEPS - 1) as i:
                final_step(i)
            final_step(D_STEPS - 1, last=True)
            for k in range(2):
                sp.wait_ge(s_out[k], AHEAD + 16 * D_STEPS * UNITS // 2)

        @block.gpsimd
        def _(pool):
            nc.gpsimd.memset(ident[:, :], 0.0).then_inc(s_ident, 1)
            nc.gpsimd.memset(ones[:, :], 1.0).then_inc(s_ident, 1)
            nc.gpsimd.memset(ones_row[:, :], 1.0).then_inc(s_ident, 1)
            nc.gpsimd.memset(one8[:, :], 1.0).then_inc(s_ident, 1)
            for e in range(E):
                nc.gpsimd.memset(kio[:, e:e + 1], float(e + 1)).then_inc(s_ident, 1)
            for s in (s_hw, s_hwT, s_hwl, s_hwtp, s_z, s_acc, *s_gst, *s_out):
                nc.gpsimd.nop().then_inc(s, AHEAD)
            for tab in (mean, rs):
                nc.gpsimd.memset(tab[:, :, :], 0.0).then_inc(s_ident, 1)
            pool.wait_ge(s_ident, 6 + E)
            nc.gpsimd.affine_select(out=ident[:, :], in_=ident[:, :], compare_op=ALU.not_equal, fill=1.0,
                                    base=0, pattern=[[-1, P]], channel_multiplier=1).then_inc(s_ident, 1)
            for n in range(2):
                pool.wait_ge(s_tp, G_X2 - 4 * n)
                nc.gpsimd.memset(acc[n], 0.0).then_inc(s_acc0, 1)

        IDENT = 7 + E

        def item_dst(w, a, m, q):
            if m >= IT_W:
                return w[:, 4 * q:4 * q + 4, (m - IT_W) * P:(m - IT_W + 1) * P]
            return a[:, 4 * q:4 * q + 4, 0:ER]

        def item_group(m):
            return G_AT if m == IT_AT else G_W + 4 * (m - IT_W)

        def x_group(T):
            return (G_X0, G_X1, G_X2)[T]

        @block.scalar
        def _(act):
            def row_sums(m, halves=(0, 1)):
                np_ = E if m == IT_R else P
                if 0 in halves:
                    if m == IT_AT:
                        act.wait_ge(s_at, 1)
                    else:
                        act.wait_ge(s_item[m % 4], 16 * (m // 4 + (m % 4 != IT_AT)))
                for h in halves:
                    part = slice(h * HALF, (h + 1) * HALF)
                    if m == IT_AT:
                        spare = a_lo[:, part, 0:ER]
                    else:
                        at = (m - IT_W if m >= IT_W else WT - 1) * P
                        spare = w_lo[0:np_, part, at:at + P]
                    nc.scalar.activation(spare, stage[m % 4][0:np_, :].rearrange("p (k c) -> p k c", k=KB)[:, part, :],
                                         ACT.Abs, accum_out=l1[0:np_, h, m:m + 1]).then_inc(s_l1, 1)

            def root():
                nc.scalar.activation(std[:, :], vare[:, :], ACT.Sqrt).then_inc(s_std, 1)

            def evacuate(dst, q, group):
                act.wait_ge(s_tp, group + 1)
                nc.scalar.activation(dst, tp_bank(q, group)[:, :].rearrange("p (k r) -> p k r", k=4), ACT.Copy)\
                    .then_inc(s_hi, 1)

            def item_hi(m):
                for q in range(4):
                    evacuate(item_dst(w_hi, a_hi, m, q), q, item_group(m) + q)
                    if q % 2 == 1 and m + 2 < ITEMS:
                        row_sums(m + 2, (q // 2,))

            def hi_part(n, q, group):
                evacuate(xt_hi[:, n, 4 * q:4 * q + 4, :], q, group)

            def hwT_out(T, n):
                act.wait_ge(s_hwtp, AHEAD + T + 1)
                nc.scalar.activation(hwT[:, n, 0, :], hwb[0:ER, 0:P], ACT.Copy).then_inc(s_hwT, 1)

            def silu(count, b):
                act.wait_ge(s_zb, count + 1)
                nc.scalar.activation(zs[:, b, :], zs[:, b, :], ACT.Silu).then_inc(s_g, 1)

            def store_g(count, b, n, j, q):
                act.wait_ge(s_g, count + 1)
                act.dma_start(g_dram[ds(j * P + n * B_PAIRS * P, P), cols(q)], zs[:, b, :]).then_inc(s_gst[b], 16)

            row_sums(IT_R)
            act.wait_ge(s_rt, 1)
            nc.scalar.activation(a_hi[:, :, ER:AUG], hb[:, 0:P].rearrange("p (k e) -> p k e", e=E), ACT.Copy)\
                .then_inc(s_rhi, 1)
            act.wait_ge(s_var, 1)
            root()
            for q in range(4):
                hi_part(0, q, G_X0 + q)
            row_sums(IT_W)
            for q in range(4):
                hi_part(1, q, G_X1 + q)
                if q == 1:
                    row_sums(IT_AT)
            act.wait_ge(s_const, 16)
            nc.scalar.activation(abs_b, raw_b, ACT.Abs).then_inc(s_absb, 1)
            item_hi(IT_AT)
            for m in range(IT_W, ITEMS):
                item_hi(m)
                c, place = divmod(m - IT_W - 4, 4)
                if c == 0 and place < 2:
                    hwT_out(place, place)
                if c >= 1 and place < 2:
                    silu(2 * (c - 1) + place, place)
                    store_g(2 * (c - 1) + place, place, place, 0, c - 1)

            def pair_root(p):
                act.wait_ge(s_var, p + 1)
                root()

            def pair_norm(order, scale=r2, offset=std):
                for n in range(2):
                    nc.scalar.activation(xp[n], xp[n], ACT.Identity, scale=scale[:, n:n + 1],
                                         bias=offset[:, n:n + 1]).then_inc(s_xnp, 1)

            pair_root(1)
            act.wait_ge(s_rstd, 2)
            pair_norm(0)
            for n in range(2):
                silu(4 + n, n)
                store_g(4 + n, n, n, 0, 2)
            act.wait_ge(s_z, AHEAD + 7)
            for q in range(4):
                hi_part(0, q, G_X2 + q)
            for n in range(2):
                silu(6 + n, n)
                store_g(6 + n, n, n, 0, 3)

            def early_tile(i, n, first=False, carry=False, late=False, last=False):
                T = 2 * i + n
                p = B_STATS * i + n

                def hi(q):
                    hi_part(1 - n, q, TB + 4 * (T + 1) + q)

                def norm_stats():
                    pair_root(p)
                    act.wait_ge(s_rstd, p + 1)
                    pair_norm(p)

                if first:
                    act.wait_ge(s_z, AHEAD + 4 * T)
                    hi(0)
                    hwT_out(T, n)
                    act.wait_ge(s_xp, 64)
                    pair_norm(1, rstd[:, :, 0], nmr[:, :, 0])
                    hi(1)
                else:
                    if not late:
                        norm_stats()
                    act.wait_ge(s_z, AHEAD + 4 * T)
                    hi(0)
                    hwT_out(T, n)
                    if late and not carry:
                        norm_stats()
                    hi(1)
                    if carry:
                        norm_stats()
                if last:
                    act.wait_ge(s_d, 1)
                    nc.scalar.activation(ex[:, :], ex[:, :], ACT.Exp).then_inc(s_e, 1)
                hi(2)
                silu(4 * T, 0)
                silu(4 * T + 1, 1)
                store_g(4 * T, 0, n, i, 0)
                store_g(4 * T + 1, 1, n, i, 1)
                hi(3)
                if first:
                    norm_stats()
                silu(4 * T + 2, 0)
                store_g(4 * T + 2, 0, n, i, 2)
                silu(4 * T + 3, 1)
                store_g(4 * T + 3, 1, n, i, 3)

            def load_ahead(j, n, q):
                act.dma_start(xc[:, q, :], xr[rows(n, j), cols(q)]).then_inc(s_xc[q], 16)

            early_tile(1, 0, first=True)
            early_tile(1, 1, carry=True, late=True)
            for n in range(2):
                early_tile(2, n, late=True)
            with act.Fori(3, B_PAIRS - 1) as i:
                for n in range(2):
                    early_tile(i, n)
            early_tile(B_PAIRS - 1, 0)
            early_tile(B_PAIRS - 1, 1, last=True)

            def norm_unit(i, k):
                n, j, q, _ = unit_place(i, units[k])
                b = k % 2
                act.wait_ge(s_fl[b], total[b] * i + load_count[k])
                act.wait_ge(s_out[b], AHEAD + 16 * (UNITS // 2 * i + k // 2))
                f = pair_tab[:, 0 if units[k][0] == "early" else 1]
                nc.scalar.activation(na[b], xa[b], ACT.Identity, scale=f[:, 0, n:n + 1], bias=f[:, 1, n:n + 1])
                nc.scalar.activation(xo[b], xo[b], ACT.Identity, scale=f[:, 0, 1 - n:2 - n],
                                     bias=f[:, 1, 1 - n:2 - n]).then_inc(s_nrm, 1)

            def pair_columns(slot, j):
                act.drain()
                nc.scalar.copy(pair_tab[:, slot, 0, :], rstd[:, :, ds(j, 1)].rearrange("p n a -> p (n a)"))
                nc.scalar.copy(pair_tab[:, slot, 1, :], nmr[:, :, ds(j, 1)].rearrange("p n a -> p (n a)"))
                act.drain()

            def final_step(i, last=False):
                pair_columns(0, i)
                for t in range(TILES_D):
                    T, j, n = tile_of(i, t)
                    if n == 0:
                        pair_columns(1, j)
                    e0, e1, f0, f1, f2, f3 = per_tile[t]

                    def norms(group):
                        for k in group:
                            norm_unit(i, k)

                    def hi(q):
                        if last and t == TILES_D - 1:
                            return
                        hi_part(1 - n, q, TB + PX + 4 * (T + 1) + q)
                        if q >= 2 and not (last and t >= TILES_D - 2):
                            load_ahead(j + 1, n, q - 2)

                    norms(e0)
                    act.wait_ge(s_z, AHEAD + 4 * T)
                    hi(0)
                    hwT_out(T, n)
                    norms(e1)
                    hi(1)
                    norms(f0)
                    silu(4 * T, 0)
                    silu(4 * T + 1, 1)
                    hi(2)
                    norms(f1)
                    hi(3)
                    norms(f2)
                    silu(4 * T + 2, 0)
                    norms(f3)
                    silu(4 * T + 3, 1)

            with act.Fori(0, D_STEPS - 1) as i:
                final_step(i)
            final_step(D_STEPS - 1, last=True)

        @block.vector
        def _(dve):
            v = nc.vector

            def row_stats(src):
                for n in range(2):
                    for q in range(NQ):
                        v.bn_stats(bn[:, n, q, :], src[n][:, cols(q)])
                dve.drain()
                for n in range(2):
                    v.bn_aggr(mv[:, n, :], bn[:, n, :, :])
                dve.drain()
                v.tensor_scalar(vare[:, :], mv[:, :, 1], EPS, None, ALU.add).then_inc(s_var, 1)

            def row_tables(j, count):
                dve.wait_ge(s_std, count)
                v.reciprocal(r2[:, :], std[:, :])
                dve.drain()
                v.scalar_tensor_tensor(out=std[:, :], in0=mv[:, :, 0], scalar=-1.0, in1=r2[:, :],
                                       op0=ALU.mult, op1=ALU.mult)
                v.tensor_copy(mean[:, :, ds(j, 1)].rearrange("p n a -> p (n a)"), mv[:, :, 0])
                v.tensor_scalar(rs[:, :, ds(j, 1)].rearrange("p n a -> p (n a)"), r2[:, :], XS, None, ALU.mult)
                v.tensor_copy(rstd[:, :, ds(j, 1)].rearrange("p n a -> p (n a)"), r2[:, :])
                dve.drain()
                v.tensor_copy(nmr[:, :, ds(j, 1)].rearrange("p n a -> p (n a)"), std[:, :]).then_inc(s_rstd, 1)

            def scale_of(m):
                np_ = E if m == IT_R else P
                one = slice(m, m + 1)
                dve.wait_ge(s_l1, 2 * {IT_R: 1, IT_W: 2, IT_AT: 3}.get(m, m))
                if m < IT_W:
                    v.tensor_scalar(l1[0:np_, 0, one], l1[0:np_, 0, one], l1[0:np_, 1, one], 2.0 ** -100,
                                    ALU.add, ALU.max)
                else:
                    if m == IT_W:
                        dve.wait_ge(s_bound, 1)
                        v.tensor_scalar(extra[:, :], hb[:, 0:WT], 2.0 ** -100, None, ALU.max).then_inc(s_rowu, 1)
                        dve.drain()
                    v.tensor_scalar(l1[:, 0, one], l1[:, 0, one], l1[:, 1, one], extra[:, m - IT_W:m - IT_W + 1],
                                    ALU.add, ALU.add)
                dve.drain()
                if m == IT_AT:
                    v.tensor_copy(l1_at[:, :], l1[:, 0, one])
                v.tensor_scalar(eb[0:np_, one], l1[0:np_, 0, one].bitcast(U32), 0xFF * EXP, None, ALU.bitwise_and)
                dve.drain()
                v.tensor_scalar(sc[0:np_, one], eb[0:np_, one], -1.0, float((2 * 127 + 14) * EXP), ALU.mult, ALU.add)
                v.tensor_scalar(us[0:np_, one], eb[0:np_, one], float(-(14 + 8) * EXP), None, ALU.add)
                dve.drain()
                v.tensor_scalar(isc[0:np_, one], sc[0:np_, one].bitcast(F32), XS, None, ALU.mult)

            def scale_half(m, h):
                np_ = E if m == IT_R else P
                half = stage[m % 4][0:np_, h * L // 2:(h + 1) * L // 2]
                v.tensor_scalar(half, half, sc[0:np_, m:m + 1].bitcast(F32), None, ALU.mult).then_inc(s_scaled, 1)

            def scale_item(m):
                scale_of(m)
                scale_half(m, 0)
                scale_half(m, 1)

            def norm_raw(n, q):
                v.tensor_scalar(xc[:, q % 2, :], raw0[n][:, cols(q)], mean[:, n, 0:1], rs[:, n, 0:1],
                                ALU.subtract, ALU.mult).then_inc(s_xn, 1)

            def norm_chunk(T, j, n, q):
                dve.wait_ge(s_xc[q % 2], 16 * (2 * (T - 2) + q // 2 + 1))
                v.tensor_scalar(xc[:, q % 2, :], xc[:, q % 2, :], mean[:, n, ds(j, 1)], rs[:, n, ds(j, 1)],
                                ALU.subtract, ALU.mult).then_inc(s_xn, 1)

            def split(dst, hi, q, count):
                dve.wait_ge(s_hi, count)
                bank = tp_bank(q, count + 3)
                v.tensor_tensor(dst, bank[:, :].rearrange("p (k r) -> p k r", k=4), hi, ALU.subtract)\
                    .then_inc(s_lo, 1)

            def lo_part(n, q, count):
                split(xt_lo[:, n, 4 * q:4 * q + 4, :], xt_hi[:, n, 4 * q:4 * q + 4, :], q, count)

            def item_lo(m, between):
                for q in range(4):
                    split(item_dst(w_lo, a_lo, m, q), item_dst(w_hi, a_hi, m, q), q, item_group(m) + q + 1 - 4)
                    if q < 3 and m + 1 < ITEMS:
                        scale_of(m + 1) if q == 0 else scale_half(m + 1, q - 1)
                    for slot, work_, *args in between:
                        if slot == q:
                            work_(*args)

            def build_diag(slot, columns):
                for a, (col, np_) in enumerate(columns):
                    v.tensor_scalar(slot[0:np_, a * P:a * P + np_], ident[0:np_, 0:np_], col, None, ALU.mult)
                dve.drain()
                v.memset(sp_n[:, :], 0.0).then_inc(s_diag, 1)

            def build_rows(c):
                if c:
                    dve.wait_ge(s_row, 2 * c + 1)
                for k, table in enumerate((us[:, :].bitcast(F32), isc[:, :])):
                    build_diag(diag_row[k], [(table[:, IT_W + 4 * c + a:IT_W + 4 * c + a + 1], P) for a in range(4)])

            def read_rows(c):
                dve.wait_ge(s_row, 2 * c + 2)
                v.tensor_copy(unscale[:, cols(c)], row_bank(c, 0)[:, :]).then_inc(s_rowu, 1)
                dve.wait_ge(s_row, 2 * c + 3)
                v.tensor_tensor(diag[0], raw_b[:, cols(c)], row_bank(c, 1)[:, :], ALU.mult)
                dve.drain()
                v.tensor_copy(b_lora[:, c, 0, :], diag[0])
                dve.drain()
                v.tensor_tensor(b_lora[:, c, 1, :], diag[0], b_lora[:, c, 0, :], ALU.subtract).then_inc(s_rowu, 1)
                dve.drain()

            def hw_lo(T, n):
                dve.wait_ge(s_hwT, AHEAD + T + 1)
                v.tensor_tensor(hwT[:, n, 1, :], hwb[0:ER, 0:P], hwT[:, n, 0, :], ALU.subtract).then_inc(s_hwl, 1)

            scale_item(IT_R)
            dve.wait_ge(s_x0, 32)
            row_stats(raw0)
            dve.wait_ge(s_ident, IDENT)
            row_tables(0, 1)
            dve.drain()
            norm_raw(0, 0)
            norm_raw(0, 1)
            dve.wait_ge(s_item[IT_A], 16)
            v.tensor_copy(a_grouped.rearrange("p (k e r) -> p k e r", k=KB, e=E),
                          stage[IT_A].rearrange("p (e k r) -> p k e r", e=E, k=KB)).then_inc(s_ag, 1)
            dve.wait_ge(s_rhi, 1)
            v.tensor_tensor(a_lo[:, :, ER:AUG], hb[:, 0:P].rearrange("p (k e) -> p k e", e=E),
                            a_hi[:, :, ER:AUG], ALU.subtract).then_inc(s_rowu, 1)
            for q in range(4):
                lo_part(0, q, G_X0 + q + 1)
                if q < 2:
                    norm_raw(0, q + 2)
            norm_raw(1, 0)
            norm_raw(1, 1)
            at = stage[IT_AT].rearrange("a (p k) -> a k p", k=KB)
            for q in range(4):
                dve.wait_ge(s_tp, G_A + q + 1)
                v.tensor_copy(at[:, 4 * q:4 * q + 4, :], tp_bank(q, G_A)[:, :].rearrange("p (k o) -> p k o", k=4))\
                    .then_inc(s_lo, 1)
            dve.drain()
            v.memset(sp_n[:, :], 0.0).then_inc(s_at, 1)
            for q in range(4):
                lo_part(1, q, G_X1 + q + 1 - 4)
                if q < 2:
                    norm_raw(1, q + 2)
            scale_item(IT_AT)
            dve.drain()
            build_diag(diag_row[0], [(us[0:E, IT_R:IT_R + 1].bitcast(F32), E)])
            dve.wait_ge(s_absb, 1)
            v.memset(unscale_aug[:, 0:ER], H_UNSCALE)
            v.tensor_scalar(raw_b, raw_b, us[:, IT_AT:IT_AT + 1].bitcast(F32), 1.0 / H_UNSCALE, ALU.mult, ALU.mult)
            item_lo(IT_AT, [])
            dve.wait_ge(s_row, 1)
            v.tensor_copy(unscale_aug[:, ER:AUG], hb[:, ER:AUG]).then_inc(s_rowu, 1)
            dve.drain()

            def mix_h(T):
                dve.wait_ge(s_h, T + 1)
                dve.wait_ge(s_hwtp, AHEAD + T)
                v.tensor_tensor(haug[:, :], hb[:, 0:AUG], unscale_aug[:, :], ALU.mult)
                dve.drain()
                v.tensor_tensor(sp_z[:, :], haug[:, ER:AUG], bias_r[:, :], ALU.add)
                dve.drain()
                v.max(sp_s[:, :], sp_z[:, :])
                dve.drain()
                v.tensor_tensor_scan(sp_c[:, :], one8[:, :], sp_s[:, :], 0.0, ALU.mult, ALU.add)
                v.tensor_tensor(sp_k[:, :], sp_s[:, :], kio[:, :], ALU.mult)
                dve.drain()
                v.scalar_tensor_tensor(out=sp_u[:, :], in0=sp_k[:, :], scalar=1.0, in1=sp_c[:, :],
                                       op0=ALU.add, op1=ALU.is_gt, accum_out=sp_n[:, 0:1])
                dve.drain()
                v.scalar_tensor_tensor(out=sp_v[:, :], in0=sp_s[:, :], scalar=1.0, in1=sp_u[:, :],
                                       op0=ALU.mult, op1=ALU.mult, accum_out=sp_n[:, 1:2])
                v.reciprocal(sp_n[:, 2:3], sp_n[:, 0:1])
                dve.drain()
                v.tensor_scalar(sp_n[:, 3:4], sp_n[:, 1:2], -1.0, sp_n[:, 2:3], ALU.add, ALU.mult)
                dve.drain()
                v.tensor_scalar(sp_w[:, :], sp_z[:, :], sp_n[:, 3:4], 0.0, ALU.subtract, ALU.max)
                dve.drain()
                v.tensor_tensor(hw[:, :].rearrange("p (e r) -> p e r", e=E),
                                haug[:, 0:ER].rearrange("p (e r) -> p e r", e=E),
                                sp_w[:, :].rearrange("p (e a) -> p e a", a=1).to_broadcast([P, E, R]),
                                ALU.mult).then_inc(s_hw, 1)

            def z_out(chunks):
                for count, bank, q, b in chunks:
                    dve.wait_ge(s_z, AHEAD + count + 1)
                    v.tensor_tensor(zs[:, b, :], zb[bank][:, :], unscale[:, cols(q)], ALU.mult).then_inc(s_zused, 1)
                dve.drain()
                for count, bank, q, b in chunks:
                    v.tensor_tensor(zs[:, b, :], zs[:, b, :], bias[:, cols(q)], ALU.add).then_inc(s_zb, 1)

            def first_z_out(c, n):
                if c == 0 and n == 0:
                    dve.wait_ge(s_bias, 16)
                if c:
                    dve.wait_ge(s_gst[n], AHEAD + 16 * c)
                z_out([(2 * c + n, 2 * (c % 2) + n, c, n)])

            def g_stored(T, q):
                dve.wait_ge(s_gst[q % 2], AHEAD + 16 * (2 * T + q // 2))

            dve.wait_ge(s_bias_r, 16)
            for m in range(IT_W, ITEMS):
                c, place = divmod(m - IT_W - 4, 4)
                between = []
                if c == 0 and place < 2:
                    between.append((1, mix_h, place))
                if c == 0 and place in (1, 2):
                    between.insert(0, (0, hw_lo, place - 1, place - 1))
                if c >= 1 and place < 2:
                    between.append((1, first_z_out, c - 1, place))
                if place == 2:
                    between.append((3, build_rows, c + 1))
                if place == 3:
                    between.append((3, read_rows, c + 1))
                item_lo(m, between)


            def pair_stats(p, order):
                dve.wait_ge(s_xp, 32 * order + 32)
                row_stats(xp)
                row_tables(p, p + 1)

            def pair_sums(order, half):
                part = slice(half * 1024, half * 1024 + 1024)
                if half == 0:
                    dve.wait_ge(s_xnp, 2 * order + 2)
                v.tensor_tensor(dtmp, xp[1][:, part], xp[0][:, part], ALU.subtract)
                dve.drain()
                v.tensor_tensor(xp[0][:, part], xp[0][:, part], dtmp, ALU.mult)
                v.tensor_tensor(xp[1][:, part], xp[1][:, part], dtmp, ALU.mult)
                dve.drain()
                v.tensor_tensor(acc[0][:, part], acc[0][:, part], xp[0][:, part], ALU.add)
                last = v.tensor_tensor(acc[1][:, part], acc[1][:, part], xp[1][:, part], ALU.subtract)
                if half == 1:
                    dve.drain()
                    v.memset(sp_v[:, :], 0.0).then_inc(s_acc, 1)

            pair_stats(1, 0)
            dve.drain()
            norm_chunk(2, 1, 0, 0)
            norm_chunk(2, 1, 0, 1)
            first_z_out(2, 0)
            first_z_out(2, 1)
            lo_part(0, 0, HB + 4 * 2 + 1)
            norm_chunk(2, 1, 0, 2)
            lo_part(0, 1, HB + 4 * 2 + 2)
            norm_chunk(2, 1, 0, 3)
            lo_part(0, 2, HB + 4 * 2 + 3)
            lo_part(0, 3, HB + 4 * 2 + 4)
            first_z_out(3, 0)
            dve.wait_ge(s_acc0, 2)
            pair_sums(0, 0)
            norm_chunk(3, 1, 1, 0)
            norm_chunk(3, 1, 1, 1)
            first_z_out(3, 1)
            pair_sums(0, 1)

            def exponents():
                dve.wait_ge(s_dsum, 1)
                v.tensor_scalar(dcol[:, :], dsum, float(C) ** -0.5, None, ALU.mult)
                dve.drain()
                v.tensor_scalar(ex[:, 0:2 * KB], dcol[:, :], 0.0, -1.0, ALU.max, ALU.mult)
                dve.drain()
                v.tensor_tensor(ex[:, 2 * KB:4 * KB], dcol[:, :], ex[:, 0:2 * KB], ALU.add).then_inc(s_d, 1)

            def p_columns():
                dve.wait_ge(s_e, 1)
                v.tensor_tensor(dcol[:, :], ex[:, 0:2 * KB], ex[:, 2 * KB:4 * KB], ALU.add)
                dve.drain()
                v.reciprocal(dcol[:, :], dcol[:, :])
                dve.drain()
                v.tensor_tensor(dcol[:, :], dcol[:, :], ex[:, 2 * KB:4 * KB], ALU.mult)
                dve.drain()

            def p_row(g):
                dve.wait_ge(s_tp, TB + 4 * (B_TILES + 1) + g + 1)
                v.tensor_copy(prow[g // NQ][:, cols(g % NQ)], tp[g % 2][:, :]).then_inc(s_lo, 1)

            def p_rows():
                for g in range(2 * NQ):
                    if g >= 2:
                        p_row(g - 2)
                    for a in range(BPQ):
                        v.tensor_scalar(diag[g % 2][:, a * P:(a + 1) * P], ident[:, :],
                                        dcol[:, BPQ * g + a:BPQ * g + a + 1], None, ALU.mult)
                    dve.drain()
                    v.memset(sp_n[:, :], 0.0).then_inc(s_diag, 1)
                p_row(2 * NQ - 2)
                p_row(2 * NQ - 1)
                dve.drain()
                v.memset(sp_n[:, :], 0.0).then_inc(s_fin, fin0)
                dve.drain()

            def early_tile(i, n, first=False, carry=False, late=False, last=False):
                T = 2 * i + n
                nj, nn = next_of(i, n)
                p = B_STATS * i + n

                def lo(q):
                    lo_part(nn, q, HB + 4 * (T + 1) + q + 1)

                def stats():
                    pair_stats(p, p)
                    dve.drain()

                mix_h(T)
                if carry:
                    pair_sums(2, 1)
                elif not first and not late:
                    stats()
                    pair_sums(p, 0)
                lo(0)
                norm_chunk(T + 1, nj, nn, 2)
                hw_lo(T, n)
                if first:
                    pair_sums(1, 0)
                elif late and not carry:
                    stats()
                    pair_sums(p, 0)
                elif not late:
                    pair_sums(p, 1)
                lo(1)
                norm_chunk(T + 1, nj, nn, 3)
                if carry:
                    stats()
                if first:
                    pair_sums(1, 1)
                if last:
                    exponents()
                lo(2)
                if last:
                    p_columns()
                g_stored(T, 0)
                g_stored(T, 1)
                z_out([(4 * T, 0, 0, 0), (4 * T + 1, 1, 1, 1)])
                lo(3)
                if carry:
                    pair_sums(p, 0)
                if late:
                    pair_sums(p, 1)
                if last:
                    p_rows()
                if first:
                    pair_stats(p, p)
                    dve.drain()
                norm_chunk(T + 2, i + 1, n, 0)
                g_stored(T, 2)
                z_out([(4 * T + 2, 2, 2, 0)])
                norm_chunk(T + 2, i + 1, n, 1)
                if first:
                    pair_sums(p, 0)
                g_stored(T, 3)
                z_out([(4 * T + 3, 3, 3, 1)])

            early_tile(1, 0, first=True)
            early_tile(1, 1, carry=True, late=True)
            for n in range(2):
                early_tile(2, n, late=True)
            with dve.Fori(3, B_PAIRS - 1) as i:
                for n in range(2):
                    early_tile(i, n)
            early_tile(B_PAIRS - 1, 0)
            early_tile(B_PAIRS - 1, 1, last=True)

            def finish(i, k):
                kind, _t, _q = units[k]
                n, j, q, T = unit_place(i, units[k])
                b = k % 2
                dve.wait_ge(s_nrm, UNITS * i + k + 1)
                v.tensor_tensor(xo[b], xo[b], na[b], ALU.subtract)
                dve.drain()
                v.tensor_tensor(xo[b], xo[b], prow[n][:, cols(q)], ALU.mult)
                dve.drain()
                v.scalar_tensor_tensor(out=na[b], in0=na[b], scalar=2.0, in1=xo[b], op0=ALU.mult, op1=ALU.add)
                dve.drain()
                if kind == "tile":
                    dve.wait_ge(s_g, 4 * T + q + 1)
                v.tensor_tensor(na[b], na[b], gx[b] if kind == "early" else zs[:, q % 2, :], ALU.mult)
                dve.drain()
                v.tensor_tensor(na[b], na[b], xa[b], ALU.add).then_inc(s_fin, 1)

            def final_step(i, last=False):
                for t in range(TILES_D):
                    T, j, n = tile_of(i, t)
                    nj, nn = next_of(j, n)
                    e0, e1, f0, f1, f2, f3 = per_tile[t]

                    def finishes(group):
                        for k in group:
                            finish(i, k)

                    def next_lo(q):
                        if last and t == TILES_D - 1:
                            return
                        lo_part(nn, q, HB + 4 * (T + 1) + q + 1)
                        if q < 2:
                            norm_chunk(T + 1, nj, nn, q + 2)

                    def norm_ahead(q):
                        if not (last and t >= TILES_D - 2):
                            norm_chunk(T + 2, j + 1, n, q)

                    mix_h(T)
                    finishes(e0)
                    next_lo(0)
                    hw_lo(T, n)
                    finishes(e1)
                    next_lo(1)
                    z_out([(4 * T, 0, 0, 0), (4 * T + 1, 1, 1, 1)])
                    finishes(f0)
                    next_lo(2)
                    finishes(f1)
                    next_lo(3)
                    z_out([(4 * T + 2, 2, 2, 0)])
                    norm_ahead(0)
                    finishes(f2)
                    norm_ahead(1)
                    z_out([(4 * T + 3, 3, 3, 1)])
                    finishes(f3)

            with dve.Fori(0, D_STEPS - 1) as i:
                final_step(i)
            final_step(D_STEPS - 1, last=True)

        @block.tensor
        def _(pe):
            mm = nc.tensor.matmul

            def transpose_group(q, src, group):
                bank = tp_bank(q, group)
                if not isinstance(group, int) or group >= WIDE:
                    pe.wait_ge(s_lo, group - 1)
                elif group >= 4:
                    pe.wait_ge(s_lo, group - 3)
                for a in range(4):
                    last = nc.tensor.transpose(bank[:, a * P:(a + 1) * P], src[:, a * P:(a + 1) * P], ident[:, :])
                last.then_inc(s_tp, 1)

            def transpose_chunk(T, q, group):
                pe.wait_ge(s_xn, 4 * T + q + 1)
                transpose_group(q, xc[:, q % 2, :], group)

            def passes(n, k):
                return ((xt_hi[:, n, k, :], 0), (xt_hi[:, n, k, :], 1), (xt_lo[:, n, k, :], 0))

            def hidden(n):
                for k in range(KB):
                    for a, (lhs, w) in enumerate(passes(n, k)):
                        last = mm(hb[:, 0:AUG], lhs, (a_hi, a_lo)[w][:, k, :], start=(k == 0 and a == 0),
                                  stop=(k == KB - 1 and a == 2))
                last.then_inc(s_h, 1)

            def base(bank, n, c, ks):
                for k in ks:
                    for a, (lhs, w) in enumerate(passes(n, k)):
                        mm(zb[bank][:, :], lhs, (w_hi, w_lo)[w][:, k, cols(c)], start=(k == 0 and a == 0), stop=False)

            def lora(bank, n, c):
                for h, b in ((0, 0), (0, 1), (1, 0)):
                    last = mm(zb[bank][:, :], hwT[:, n, h, :], b_lora[:, c, b, :], start=False, stop=(h == 1))
                last.then_inc(s_z, 1)

            def transpose_hw(T):
                pe.wait_ge(s_hw, AHEAD + T + 1)
                pe.wait_ge(s_hwl, AHEAD + T)
                nc.tensor.transpose(hwb[0:ER, 0:P], hw[:, :], ident[:, :]).then_inc(s_hwtp, 1)

            def item_group_pe(m, q):
                if q % 2 == 0:
                    pe.wait_ge(s_scaled, (3 if m == IT_AT else 2 * (m - IT_W) + 5) + q // 2)
                transpose_group(q, stage[m % 4][:, 4 * q * P:4 * (q + 1) * P], item_group(m) + q)

            def make_rows(c):
                for k in range(2):
                    pe.wait_ge(s_diag, 2 + 2 * c + k)
                    if c == 0 and k == 1:
                        pe.wait_ge(s_rowu, 4)
                    mm(row_bank(c, k)[:, :], ones_row[:, :], diag_row[k], start=True, stop=True).then_inc(s_row, 1)

            pe.wait_ge(s_ident, IDENT)
            pe.wait_ge(s_scaled, 2)
            for k in range(KB):
                last = nc.tensor.transpose(hb[:, k * E:(k + 1) * E], stage[IT_R][0:E, k * P:(k + 1) * P],
                                           ident[0:E, 0:E])
            last.then_inc(s_rt, 1)
            for q in range(4):
                transpose_chunk(0, q, G_X0 + q)
            pe.wait_ge(s_ag, 1)
            for q in range(4):
                transpose_group(q, a_grouped[:, 4 * q * P:4 * (q + 1) * P], G_A + q)
            for q in range(4):
                transpose_chunk(1, q, G_X1 + q)
            pe.wait_ge(s_absb, 1)
            pe.wait_ge(s_scaled, 3)
            pe.wait_ge(s_rowu, 1)
            for m in range(WT):
                last = mm(hb[:, m:m + 1], abs_b[:, m * P:(m + 1) * P], l1_at[:, :], start=True, stop=True)
            last.then_inc(s_bound, 1)
            for q in range(4):
                item_group_pe(IT_AT, q)
            pe.wait_ge(s_diag, 1)
            pe.wait_ge(s_rowu, 2)
            mm(hb[:, ER:AUG], ones_row[0:E, :], diag_row[0][0:E, 0:E], start=True, stop=True).then_inc(s_row, 1)
            for m in range(IT_W, IT_W + 4):
                for q in range(4):
                    item_group_pe(m, q)
            pe.wait_ge(s_rowu, 3)
            hidden(0)
            make_rows(0)
            pe.wait_ge(s_lo, G_W + 16)

            for c in range(NQ - 1):
                banks = [2 * (c % 2) + n for n in range(2)]
                if c == 1:
                    pe.wait_ge(s_lo, WIDE)
                if c == 2:
                    pe.wait_ge(s_zused, 2)
                for place in range(4):
                    for q in range(4):
                        item_group_pe(IT_W + 4 * (c + 1) + place, q)
                        for n in range(2):
                            base(banks[n], n, c, [4 * place + q])
                        if place == 3 and q == 1:
                            if c == 0:
                                pe.wait_ge(s_hwl, AHEAD + 2)
                            make_rows(c + 1)
                    if c == 0 and place < 2:
                        transpose_hw(place)
                        if place == 0:
                            hidden(1)
                for n in range(2):
                    lora(banks[n], n, c)
            pe.wait_ge(s_rowu, 3 + 2 * NQ)
            pe.wait_ge(s_zused, 4)
            base(2, 0, 3, range(KB))
            lora(2, 0, 3)
            for q in range(4):
                transpose_chunk(2, q, G_X2 + q)
                base(3, 1, 3, range(4 * q, 4 * q + 4))
            lora(3, 1, 3)

            def tile(T, n, px, sums=False, last=False):
                def next_chunk(q):
                    if not last:
                        transpose_chunk(T + 1, q, TB + px + 4 * (T + 1) + q)

                def bank_free(c):
                    pe.wait_ge(s_zused, 4 * T + c - 3)

                pe.wait_ge(s_lo, TB + px + 4 * T + 4)
                pe.wait_ge(s_hw, AHEAD + T)
                hidden(n)
                bank_free(0)
                base(0, n, 0, range(KB))
                next_chunk(0)
                bank_free(1)
                base(1, n, 1, range(0, HALF))
                transpose_hw(T)
                base(1, n, 1, range(HALF, KB))
                next_chunk(1)
                bank_free(2)
                base(2, n, 2, range(0, HALF))
                if sums:
                    pe.wait_ge(s_hwl, AHEAD + T + 1)
                    pe.wait_ge(s_acc, AHEAD + PAIRS)
                    for k in range(2 * KB):
                        col = mm(dsum[:, k:k + 1], acc[k // KB][:, (k % KB) * P:(k % KB + 1) * P], ones[:, 0:1],
                                 start=True, stop=True)
                    col.then_inc(s_dsum, 1)
                next_chunk(2)
                pe.wait_ge(s_hwl, AHEAD + T + 1)
                lora(0, n, 0)
                lora(1, n, 1)
                base(2, n, 2, range(HALF, KB))
                lora(2, n, 2)
                next_chunk(3)
                bank_free(3)
                for k in range(KB):
                    base(3, n, 3, [k])
                    if sums and k % 2 == 1:
                        g = k // 2
                        pe.wait_ge(s_diag, 1 + 2 * NQ + g + 1)
                        pe.wait_ge(s_lo, TB + 4 * (B_TILES + 1) + g - 1)
                        mm(tp[g % 2][:, :], ones[:, :], diag[g % 2], start=True, stop=True).then_inc(s_tp, 1)
                lora(3, n, 3)

            with pe.Fori(1, B_PAIRS - 1) as i:
                for n in range(2):
                    tile(2 * i + n, n, 0)
            tile(B_TILES - 2, 0, 0)
            tile(B_TILES - 1, 1, 0, sums=True)
            with pe.Fori(0, D_STEPS - 1) as i:
                for t in range(TILES_D):
                    T, _j, n = tile_of(i, t)
                    tile(T, n, PX)
            for t in range(TILES_D):
                T, _j, n = tile_of(D_STEPS - 1, t)
                tile(T, n, PX, last=(t == TILES_D - 1))


def kernel(L0_attn_x, L0_ffn_W_base, L0_ffn_b_base, L0_ffn_W_router, L0_ffn_b_router, L0_ffn_lora_A, L0_ffn_lora_B):
    import numpy as np
    import concourse.bacc as bacc
    from concourse import mybir
    from concourse.bass_utils import run_bass_kernel_spmd

    nc = bacc.Bacc("TRN2", target_bir_lowering=False, num_devices=1, dynamic_dma_scratch_size=1024)
    ins = {
        "in_x": L0_attn_x, "in_w_base": L0_ffn_W_base, "in_b_base": L0_ffn_b_base, "in_w_router": L0_ffn_W_router,
        "in_b_router": L0_ffn_b_router, "in_lora_a": L0_ffn_lora_A, "in_lora_b": L0_ffn_lora_B,
    }
    ins = {k: np.ascontiguousarray(a) for k, a in ins.items()}
    args = [nc.dram_tensor(k, a.shape, mybir.dt.from_np(a.dtype), kind="ExternalInput").ap() for k, a in ins.items()]
    shape = ins["in_x"].shape
    out = nc.dram_tensor("out_0", shape, mybir.dt.float32, kind="ExternalOutput").ap()
    g_dram = nc.dram_tensor("g_early", (shape[1], shape[2]), mybir.dt.float32, kind="Internal").ap()
    build(nc, *args, out, g_dram)
    r = run_bass_kernel_spmd(nc, [ins], core_ids=[0])
    return r.results[0]["out_0"]
```
